# Optimizing a Trainium2 kernel written in Bass

```python
import numpy as np
import jax
import jax.numpy as jnp

def _softmax(x, axis=-1):
    return jax.nn.softmax(x, axis=axis)

def _gelu(x):
    return jax.nn.gelu(x, approximate=True)

def _silu(x):
    return jax.nn.silu(x)

def _sigmoid(x):
    return jax.nn.sigmoid(x)

def _layernorm(x, axis=-1, eps=1e-05):
    m = jnp.mean(x, axis=axis, keepdims=True)
    v = jnp.var(x, axis=axis, keepdims=True)
    return (x - m) / jnp.sqrt(v + eps)

def _scatter_add(tgt, idx, src, axis=0):
    return tgt.at[idx].add(src)

def _segment_sum(src, seg, n):
    return jax.ops.segment_sum(src, seg, n)
kernel_name = 'mk_gnn_resnorm_d1_gnn_r8_a19ed8'

def setup_inputs(seed: int=0):
    np.random.seed(seed)
    _w = jnp.asarray

    def _rec_inputs():
        import jax
        import jax.numpy as jnp
        _gk = jax.random.key(seed)
        x = -0.000202 + 1 * jax.random.normal(jax.random.fold_in(_gk, 1), (12500, 64), jnp.float32)
        _s = jax.random.randint(jax.random.fold_in(_gk, 2), (200000,), 0, 12500, jnp.int32)
        _d = jax.random.randint(jax.random.fold_in(_gk, 3), (200000,), 0, 12500, jnp.int32)
        _loop = jnp.arange(12500, dtype=jnp.int32)
        src = jnp.concatenate([_s, _d, _loop])
        dst = jnp.concatenate([_d, _s, _loop])
        _o = jnp.argsort(dst, stable=True)
        src = src[_o]
        dst = dst[_o]
        edge_attr_32 = 0.000164634 + 1.0002 * jax.random.normal(jax.random.fold_in(_gk, 11), (412500, 32), jnp.float32)
        return (x, src, dst, edge_attr_32)
    x, src, dst, edge_attr_32 = _rec_inputs()

    def _L0_gnn_setup():
        import jax, jax.numpy as jnp
        import numpy as np
        N_NODES = 12500
        N_EDGES = 156250
        NODE_DIM = 64
        EDGE_DIM = 32
        N_LAYERS = 3
        BN_EPS = 1e-05
        key = jax.random.key(seed)
        ks = jax.random.split(key, 8)
        x = jax.random.normal(ks[0], (N_NODES, NODE_DIM), dtype=jnp.float32)
        edge_index = jax.random.randint(ks[1], (2, N_EDGES), 0, N_NODES, dtype=jnp.int64)
        edge_attr = jax.random.normal(ks[2], (N_EDGES, EDGE_DIM), dtype=jnp.float32)
        s = 1.0 / np.sqrt(EDGE_DIM)
        edge_w = jax.random.uniform(ks[3], (N_LAYERS, EDGE_DIM, NODE_DIM), jnp.float32, -s, s)
        edge_b = jnp.zeros((N_LAYERS, NODE_DIM), jnp.float32)
        s2 = 1.0 / np.sqrt(NODE_DIM)
        mlp_w = jax.random.uniform(ks[4], (N_LAYERS, NODE_DIM, NODE_DIM), jnp.float32, -s2, s2)
        mlp_b = jnp.zeros((N_LAYERS, NODE_DIM), jnp.float32)
        gamma = jnp.ones((N_LAYERS, NODE_DIM), jnp.float32)
        beta = jnp.zeros((N_LAYERS, NODE_DIM), jnp.float32)
        return {'x': x, 'edge_index': edge_index, 'edge_attr': edge_attr, 'edge_w': edge_w, 'edge_b': edge_b, 'mlp_w': mlp_w, 'mlp_b': mlp_b, 'gamma': gamma, 'beta': beta}
    _L0_gnn_all = _L0_gnn_setup()
    _L0_gnn_in = {k: v for k, v in _L0_gnn_all.items() if k in ('edge_w', 'edge_b', 'mlp_w', 'mlp_b', 'gamma', 'beta')}
    del _L0_gnn_all
    return {'x': x, 'src': src, 'dst': dst, 'edge_attr_32': edge_attr_32, 'L0_gnn_edge_w': _L0_gnn_in['edge_w'], 'L0_gnn_edge_b': _L0_gnn_in['edge_b'], 'L0_gnn_mlp_w': _L0_gnn_in['mlp_w'], 'L0_gnn_mlp_b': _L0_gnn_in['mlp_b'], 'L0_gnn_gamma': _L0_gnn_in['gamma'], 'L0_gnn_beta': _L0_gnn_in['beta']}

def reference(x, src, dst, edge_attr_32, L0_gnn_edge_w, L0_gnn_edge_b, L0_gnn_mlp_w, L0_gnn_mlp_b, L0_gnn_gamma, L0_gnn_beta):
    import jax
    import jax.numpy as jnp

    def _L0_gnn_ref(x, edge_index, edge_attr, edge_w, edge_b, mlp_w, mlp_b, gamma, beta):
        import jax, jax.numpy as jnp
        import numpy as np
        N_NODES = 12500
        N_EDGES = 156250
        NODE_DIM = 64
        EDGE_DIM = 32
        N_LAYERS = 3
        BN_EPS = 1e-05
        src = edge_index[0]
        dst = edge_index[1]
        for l in range(N_LAYERS):
            e = edge_attr @ edge_w[l] + edge_b[l]
            msg = jax.nn.relu(x[src] + e)
            aggr = jax.ops.segment_sum(msg, dst, num_segments=N_NODES)
            h = (x + aggr) @ mlp_w[l] + mlp_b[l]
            mean = jnp.mean(h, axis=0)
            var = jnp.var(h, axis=0)
            h = (h - mean) * jax.lax.rsqrt(var + BN_EPS) * gamma[l] + beta[l]
            x = jax.nn.relu(h)
        return x
    edge_index = jnp.stack([src, dst])
    x = _layernorm(x + _L0_gnn_ref(x, edge_index, edge_attr_32, L0_gnn_edge_w, L0_gnn_edge_b, L0_gnn_mlp_w, L0_gnn_mlp_b, L0_gnn_gamma, L0_gnn_beta), axis=-1)
    return x

_drawn_inputs = setup_inputs


def setup_inputs(seed=0):
    import zlib

    import numpy as np

    out = dict(_drawn_inputs(seed))
    spreads = {'L0_gnn_edge_b': (0.0, 0.1),
     'L0_gnn_mlp_b': (0.0, 0.1),
     'L0_gnn_gamma': (1.0, 0.2),
     'L0_gnn_beta': (0.0, 0.1)}
    factors = {}
    for name, (base, spread) in spreads.items():
        noise = np.random.default_rng([zlib.crc32(name.encode()), seed]).standard_normal(out[name].shape)
        drawn = base * np.exp(spread * noise) if base else spread * noise
        out[name] = jnp.asarray(drawn.astype(out[name].dtype))
    for name, factor in factors.items():
        out[name] = (out[name] * factor).astype(out[name].dtype)
    return out
```

```python
import concourse.bass as bass
from concourse import mybir
from contextlib import ExitStack

FP32 = mybir.dt.float32
I32 = mybir.dt.int32
ALU = mybir.AluOpType
ACT = mybir.ActivationFunctionType
AX = mybir.AxisListType

P = 128
TILES = 8
GROUP = P * TILES
WINDOW = 64
LOG_WINDOW = 6
NODE_P = 100
CHUNK = 5
MASKED = -32768.0
BN_EPS = 1e-5
LN_EPS = 1e-5


def gnn_kernel(nc, x, src, dst, edge_attr, edge_w, edge_b, mlp_w, mlp_b, gamma, beta, out):
    nodes, feats = x.shape
    edges, edge_feats = edge_attr.shape
    layers = edge_w.shape[0]
    cols = nodes // NODE_P
    chunks = cols // CHUNK
    part = CHUNK * NODE_P
    rounds = chunks // CHUNK
    pairs = edges // GROUP // 2
    full = 2 * pairs
    groups = full + 1
    last_edge0 = edges - GROUP
    overlap = full * GROUP - last_edge0
    blocks = -(-full // P)
    half = TILES // 2 * edge_feats
    assert nodes == NODE_P * CHUNK * CHUNK * rounds and half == P and 0 <= overlap < GROUP
    assert 0 < full - (blocks - 1) * P < P
    padded = nodes + WINDOW

    table = nc.dram_tensor("node_table", (nodes, feats), FP32, kind="Internal").ap()
    x_rows = x.rearrange("(p c) f -> p (c f)", p=NODE_P)
    table_rows = table.rearrange("(p c) f -> p (c f)", p=NODE_P)
    out_rows = out.rearrange("(p c) f -> p (c f)", p=NODE_P)
    src_groups = src[0:full * GROUP].rearrange("(g p j) -> p g j", p=P, j=TILES)
    dst_groups = dst[0:full * GROUP].rearrange("(g p j) -> p g j", p=P, j=TILES)
    attr_groups = edge_attr[0:full * GROUP, :].rearrange("(g p j) f -> p g (j f)", p=P, j=TILES)
    src_last = src[last_edge0:edges].rearrange("(p j) -> p j", p=P)
    dst_last = dst[last_edge0:edges].rearrange("(p j) -> p j", p=P)
    attr_last = edge_attr[last_edge0:edges, :].rearrange("(p j) f -> p (j f)", p=P)

    ctx = ExitStack()
    with ctx:
        def sb(name, shape, dt=FP32):
            return ctx.enter_context(nc.sbuf_tensor(name, shape, dt))

        def sem(name):
            return ctx.enter_context(nc.semaphore(name))

        node_sum = sb("node_sum", [feats + 1, padded])
        rows = sb("rows", [NODE_P, cols * feats])
        x_keep = sb("x_keep", [NODE_P, cols * feats])
        ident = sb("ident", [P, P])
        window_nodes = sb("window_nodes", [P, WINDOW])
        last_mask = sb("last_mask", [P, TILES])
        ones_row = sb("ones_row", [1, P])
        base_all = sb("base_all", [P, groups])
        group_info = sb("group_info", [1, groups, 2], I32)
        w_edge = sb("w_edge", [P, TILES // 2 * feats])
        b_edge = sb("b_edge", [1, feats])
        w_mlp = sb("w_mlp", [feats + 1, feats])
        bn_gamma = sb("bn_gamma", [feats, 1])
        bn_beta = sb("bn_beta", [feats, 1])
        src_idx = sb("src_idx", [P, 2, TILES], I32)
        dst_idx = sb("dst_idx", [P, 2, TILES], I32)
        attr = sb("attr", [P, 2, TILES * edge_feats])
        gathered = sb("gathered", [P, 2, TILES, feats])
        attr_t = sb("attr_t", [P, 2 * P])
        summed = sb("summed", [P, TILES * feats])
        messages = sb("messages", [P, TILES, feats])
        offset = sb("offset", [P, TILES])
        onehot = sb("onehot", [P, TILES, WINDOW])
        stage = sb("stage", [feats, CHUNK, CHUNK, NODE_P])
        stats = sb("stats", [feats, chunks, 6])
        mean_var = sb("mean_var", [feats, 2])
        bn_tmp = sb("bn_tmp", [feats, 4])
        dst_rows = sb("dst_rows", [P, blocks + 1, GROUP], I32)
        bounds = sb("bounds", [P, blocks + 1, 2])
        n_windows = sb("n_windows", [P, blocks + 1], I32)
        spread_in = sb("spread_in", [P, 2, P])
        x_in = sb("x_in", [NODE_P, CHUNK, CHUNK * feats])
        ln_sq = sb("ln_sq", [NODE_P, CHUNK * CHUNK * feats])
        ln_tmp = sb("ln_tmp", [NODE_P, 4, CHUNK * CHUNK])

        ps = ctx.enter_context(nc.psum_tensor("ps", [P, 8, 512], FP32))
        ps_embed = [ps[:, 0, :], ps[:, 1, :]]
        ps_attr = ps[:, 2, 0:2 * P]
        ps_window = ps[0:feats, 3, 0:WINDOW]
        ps_ring = [ps[:, 3 + k, :] for k in range(CHUNK)]

        dst_rows_in = sem("dst_rows_in")
        x_in_in = [sem(f"x_in_in{k}") for k in range(CHUNK)]
        x_keep_in = sem("x_keep_in")
        weights_in = sem("weights_in")
        src_in = [sem(f"src_in{k}") for k in range(2)]
        dst_in = [sem(f"dst_in{k}") for k in range(2)]
        attr_in = [sem(f"attr_in{k}") for k in range(2)]
        gather_in = [[sem(f"gather_in{k}_{h}") for h in range(2)] for k in range(2)]
        table_out = sem("table_out")
        result_out = sem("result_out")
        consts_ready = sem("consts_ready")
        x_transposed = sem("x_transposed")
        bounds_ready = sem("bounds_ready")
        bounds_spread = sem("bounds_spread")
        info_ready = sem("info_ready")
        attr_transposed = sem("attr_transposed")
        attr_t_ready = sem("attr_t_ready")
        embedded = sem("embedded")
        sum_ready = sem("sum_ready")
        messages_ready = sem("messages_ready")
        onehot_ready = sem("onehot_ready")
        window_ready = sem("window_ready")
        edges_done = sem("edges_done")
        h_ready = sem("h_ready")
        h_copied = sem("h_copied")
        h_counted = sem("h_counted")
        var_ready = sem("var_ready")
        std_ready = sem("std_ready")
        norm_ready = sem("norm_ready")
        staged = sem("staged")
        rows_transposed = sem("rows_transposed")
        rows_copied = sem("rows_copied")
        node_sum_set = sem("node_sum_set")
        residual_ready = sem("residual_ready")
        square_ready = sem("square_ready")
        ln_var_ready = sem("ln_var_ready")
        ln_std_ready = sem("ln_std_ready")
        ln_ready = sem("ln_ready")
        dve_step = sem("dve_step")
        pool_step = sem("pool_step")
        sp_passed = sem("sp_passed")
        pool_passed = sem("pool_passed")
        act_passed = sem("act_passed")
        pe_passed = sem("pe_passed")
        dve_passed = sem("dve_passed")

        block = ctx.enter_context(nc.Block())

        def wait_alone(eng, s, value, passed):
            eng.wait_ge(s, value)
            eng.sem_inc(passed, 1)

        def slot_count(layer, i, k):
            return layer * (pairs + 1 - k) + i

        @block.sync
        def _(sp):
            def load_weights(layer):
                w = edge_w[bass.ds(layer, 1), :, :].rearrange("o k f -> (o k) f")
                for q in range(TILES // 2):
                    sp.dma_start(w_edge[q * edge_feats:(q + 1) * edge_feats, q * feats:(q + 1) * feats],
                                 w).then_inc(weights_in, 16)
                sp.dma_start(b_edge[:, :], edge_b[bass.ds(layer, 1), :]).then_inc(weights_in, 16)
                sp.dma_start(w_mlp[0:feats, :],
                             mlp_w[bass.ds(layer, 1), :, :].rearrange("o k f -> (o k) f")).then_inc(weights_in, 16)
                sp.dma_start(w_mlp[feats:feats + 1, :], mlp_b[bass.ds(layer, 1), :]).then_inc(weights_in, 16)
                sp.dma_start(bn_gamma[:, :],
                             gamma[bass.ds(layer, 1), :].rearrange("o f -> f o")).then_inc(weights_in, 16)
                sp.dma_start(bn_beta[:, :],
                             beta[bass.ds(layer, 1), :].rearrange("o f -> f o")).then_inc(weights_in, 16)

            def load_group(k, s, d, a):
                sp.dma_start(src_idx[:, k, :], s).then_inc(src_in[k], 16)
                sp.dma_start(dst_idx[:, k, :], d).then_inc(dst_in[k], 16)
                sp.dma_start(attr[:, k, :], a).then_inc(attr_in[k], 16)

            def group_of(view, g):
                return view[:, bass.ds(g, 1), :].rearrange("p o n -> p (o n)")

            def wait_slot(layer, i, k):
                for h in range(2):
                    wait_alone(sp, gather_in[k][h], slot_count(layer, i, k) * (8 * TILES), sp_passed)
                wait_alone(sp, attr_transposed, layer * groups + i * 2 + (k - 1), sp_passed)
                wait_alone(sp, sum_ready, layer * groups + i * 2 + (k - 1), sp_passed)

            def layer_loads(layer):
                with sp.Fori(1, pairs) as i:
                    for k in range(2):
                        g = sp.snap(i * 2 + k)
                        wait_slot(layer, i, k)
                        load_group(k, group_of(src_groups, g), group_of(dst_groups, g), group_of(attr_groups, g))
                wait_slot(layer, pairs, 0)
                load_group(0, src_last, dst_last, attr_last)
                width = CHUNK * CHUNK * feats
                with sp.Fori(0, rounds) as r:
                    at = sp.snap(r * width)
                    wait_alone(sp, rows_copied, layer * chunks + r * CHUNK + CHUNK, sp_passed)
                    sp.dma_start(table_rows[:, bass.ds(at, width)],
                                 rows[:, bass.ds(at, width)]).then_inc(table_out, 16)

            def first_groups():
                for k in range(2):
                    load_group(k, src_groups[:, k, :], dst_groups[:, k, :], attr_groups[:, k, :])

            first_groups()
            for b in range(blocks):
                n = min(P, full - b * P)
                sp.dma_start(dst_rows[0:n, b, :],
                             dst[b * P * GROUP:(b * P + n) * GROUP].rearrange("(g e) -> g e", e=GROUP)
                             ).then_inc(dst_rows_in, 16)
            sp.dma_start(dst_rows[0:1, blocks, :],
                         dst[last_edge0:edges].rearrange("(o e) -> o e", o=1)).then_inc(dst_rows_in, 16)
            sp.wait_ge(consts_ready, 1)
            load_weights(0)
            step = CHUNK * feats
            for k in range(CHUNK):
                sp.dma_start(x_in[:, k, :], x_rows[:, k * step:(k + 1) * step]).then_inc(x_in_in[k], 16)
            with sp.Fori(1, rounds) as r:
                for k in range(CHUNK):
                    at = sp.snap((r * CHUNK + k) * step)
                    wait_alone(sp, x_transposed, r * CHUNK + (k - CHUNK + 1), sp_passed)
                    sp.dma_start(x_in[:, k, :], x_rows[:, bass.ds(at, step)]).then_inc(x_in_in[k], 16)
            sp.dma_start(x_keep[:, :], x_rows).then_inc(x_keep_in, 16)

            layer_loads(0)
            with sp.Fori(1, layers) as layer:
                first_groups()
                wait_alone(sp, norm_ready, layer, sp_passed)
                load_weights(layer)
                layer_loads(layer)

            width = CHUNK * CHUNK * feats
            with sp.Fori(0, rounds) as r:
                at = sp.snap(r * width)
                wait_alone(sp, ln_ready, r + 1, sp_passed)
                sp.dma_start(out_rows[:, bass.ds(at, width)], rows[:, bass.ds(at, width)]).then_inc(result_out, 16)
            sp.wait_ge(table_out, 16 * rounds * layers)
            sp.wait_ge(result_out, 16 * rounds)

        @block.gpsimd
        def _(pool):
            nc.gpsimd.memset(w_edge[:, :], 0.0).then_inc(pool_step, 1)
            pool.wait_ge(pool_step, 1)
            pool.sem_inc(consts_ready, 1)
            nc.gpsimd.memset(ones_row[:, :], 1.0)
            nc.gpsimd.memset(last_mask[:, :], 0.0)
            nc.gpsimd.memset(ident[:, :], 0.0)
            nc.gpsimd.iota(window_nodes[:, :], [[1, WINDOW]], base=0, channel_multiplier=0,
                           allow_small_or_imprecise_dtypes=True).then_inc(pool_step, 1)
            pool.wait_ge(pool_step, 2)
            nc.gpsimd.affine_select(out=ident[:, :], in_=ident[:, :], pattern=[[-1, P]],
                                    compare_op=ALU.not_equal, fill=1.0, base=0, channel_multiplier=1)
            nc.gpsimd.affine_select(out=last_mask[:, :], in_=last_mask[:, :], pattern=[[1, TILES]],
                                    compare_op=ALU.is_ge, fill=MASKED, base=-overlap,
                                    channel_multiplier=TILES).then_inc(consts_ready, 1)

            last_node = pool.to_reg(nodes - 1)

            def gather_group(features, k):
                for j in range(TILES):
                    pool.indirect_dma_start(
                        out=gathered[:, k, j, :], out_offset=None, in_=features,
                        in_offset=bass.IndirectOffsetOnAxis(ap=src_idx[:, k, j:j + 1], axis=0),
                        bounds_check=last_node).then_inc(gather_in[k][j * 2 // TILES], 16)

            def layer_gathers(layer, features):
                for k in range(2):
                    wait_alone(pool, src_in[k], slot_count(layer, 0, k) * 16 + 16, pool_passed)
                    gather_group(features, k)
                with pool.Fori(1, pairs) as i:
                    for k in range(2):
                        wait_alone(pool, src_in[k], slot_count(layer, i, k) * 16 + 16, pool_passed)
                        wait_alone(pool, sum_ready, layer * groups + i * 2 + (k - 1), pool_passed)
                        gather_group(features, k)
                wait_alone(pool, src_in[0], slot_count(layer, pairs, 0) * 16 + 16, pool_passed)
                wait_alone(pool, sum_ready, layer * groups + (full - 1), pool_passed)
                gather_group(features, 0)

            def node_phase(layer):
                with pool.Fori(0, rounds) as r:
                    for k in range(CHUNK):
                        at = pool.snap((r * CHUNK + k) * CHUNK)
                        wait_alone(pool, staged, layer * chunks + r * CHUNK + (k + 1), pool_passed)
                        nc.gpsimd.tensor_copy(by_column[:, bass.ds(at, CHUNK), :],
                                              stage[:, k, :, :]).then_inc(node_sum_set, 1)

            by_column = node_sum[0:feats, 0:nodes].rearrange("f (p c) -> f c p", c=cols)
            layer_gathers(0, x[:, :])
            node_phase(0)
            with pool.Fori(1, layers) as layer:
                wait_alone(pool, table_out, layer * (16 * rounds), pool_passed)
                layer_gathers(layer, table[:, :])
                node_phase(layer)

        @block.scalar
        def _(act):
            by_column = node_sum[0:feats, 0:nodes].rearrange("f (p c) -> f c p", c=cols)
            with act.Fori(0, rounds) as r:
                for k in range(CHUNK):
                    at = act.snap((r * CHUNK + k) * CHUNK)
                    wait_alone(act, x_transposed, r * CHUNK + (k + 1), act_passed)
                    nc.scalar.copy(by_column[:, bass.ds(at, CHUNK), :],
                                   ps_ring[k][0:feats, 0:part].rearrange("f (c p) -> f c p", c=CHUNK)
                                   ).then_inc(node_sum_set, 1)

            def copy_attr(n):
                wait_alone(act, attr_transposed, n + 1, act_passed)
                nc.scalar.copy(attr_t[:, :], ps_attr).then_inc(attr_t_ready, 1)

            def relu_messages(n):
                wait_alone(act, sum_ready, n + 1, act_passed)
                nc.scalar.activation(messages[:, :, :].rearrange("p j f -> p (j f)"), summed[:, :],
                                     ACT.Relu).then_inc(messages_ready, 1)

            with act.Fori(0, layers) as layer:
                copy_attr(layer * groups)
                with act.Fori(0, pairs) as i:
                    for k in range(2):
                        n = layer * groups + i * 2 + k
                        copy_attr(n + 1)
                        relu_messages(n)
                relu_messages(layer * groups + full)

                with act.Fori(0, rounds) as r:
                    for k in range(CHUNK):
                        at = act.snap((r * CHUNK + k) * part)
                        wait_alone(act, h_ready, layer * chunks + r * CHUNK + (k + 1), act_passed)
                        nc.scalar.copy(node_sum[0:feats, bass.ds(at, part)],
                                       ps_ring[k][0:feats, 0:part]).then_inc(h_copied, 1)
                wait_alone(act, var_ready, layer + 1, act_passed)
                nc.scalar.activation(bn_tmp[:, 1:2], bn_tmp[:, 0:1], ACT.Sqrt).then_inc(std_ready, 1)
                wait_alone(act, norm_ready, layer + 1, act_passed)
                wait_alone(act, h_copied, layer * chunks + chunks, act_passed)

                def normalise(r, k, wait):
                    at = act.snap((r * CHUNK + k) * CHUNK)
                    if wait:
                        before = layer * chunks + r * CHUNK + (k - CHUNK + 1)
                        wait_alone(act, rows_transposed, before, act_passed)
                        wait_alone(act, node_sum_set, before + chunks, act_passed)
                    nc.scalar.activation(stage[:, k, :, :], by_column[:, bass.ds(at, CHUNK), :], ACT.Relu,
                                         bias=bn_tmp[:, 3:4], scale=bn_tmp[:, 2:3]).then_inc(staged, 1)

                for k in range(CHUNK):
                    normalise(0, k, False)
                with act.Fori(1, rounds) as r:
                    for k in range(CHUNK):
                        normalise(r, k, True)

            width = CHUNK * CHUNK * feats
            with act.Fori(0, rounds) as r:
                at = act.snap(r * width)
                wait_alone(act, residual_ready, r + 1, act_passed)
                nc.scalar.activation(ln_sq[:, :], rows[:, bass.ds(at, width)], ACT.Square).then_inc(square_ready, 1)
                wait_alone(act, ln_var_ready, r + 1, act_passed)
                nc.scalar.activation(ln_tmp[:, 2, :], ln_tmp[:, 1, :], ACT.Sqrt).then_inc(ln_std_ready, 1)

        @block.tensor
        def _(pe):
            pe.wait_ge(consts_ready, 2)

            def transpose_x(r, k, wait):
                wait_alone(pe, x_in_in[k], r * 16 + 16, pe_passed)
                if wait:
                    wait_alone(pe, node_sum_set, r * CHUNK + (k - CHUNK + 1), pe_passed)
                for c in range(CHUNK):
                    last = nc.tensor.transpose(ps_ring[k][0:feats, c * NODE_P:(c + 1) * NODE_P],
                                               x_in[:, k, c * feats:(c + 1) * feats],
                                               ident[0:NODE_P, 0:NODE_P])
                last.then_inc(x_transposed, 1)

            for k in range(CHUNK):
                transpose_x(0, k, False)
            with pe.Fori(1, rounds) as r:
                for k in range(CHUNK):
                    transpose_x(r, k, True)

            pe.wait_ge(bounds_ready, 1)
            for b in range(blocks + 1):
                n = min(P, full - b * P) if b < blocks else 1
                if b:
                    pe.wait_ge(bounds_ready, b + 1)
                for v in range(2):
                    last = nc.tensor.matmul(ps_embed[v][:, b * P:b * P + n] if b < blocks else
                                            ps_embed[v][:, full:groups],
                                            spread_in[0:n, v, :], ident[0:n, 0:n], start=True, stop=True)
                last.then_inc(bounds_spread, 1)

            def embed(n, layer, i, k):
                wait_alone(pe, attr_in[k], slot_count(layer, i, k) * 16 + 16, pe_passed)
                for q in range(2):
                    last = nc.tensor.transpose(ps_attr[:, q * P:(q + 1) * P], attr[:, k, q * half:(q + 1) * half],
                                               ident[:, :])
                last.then_inc(attr_transposed, 1)
                nc.tensor.matmul(ps_embed[k], ones_row[:, :],
                                 b_edge[:, :].unsqueeze(1).to_broadcast([1, TILES, feats]),
                                 start=True, stop=False)
                wait_alone(pe, attr_t_ready, n + 1, pe_passed)
                for q in range(2):
                    width = TILES // 2 * feats
                    last = nc.tensor.matmul(ps_embed[k][:, q * width:(q + 1) * width], attr_t[:, q * P:(q + 1) * P],
                                            w_edge[:, :], start=False, stop=(q == 1))
                last.then_inc(embedded, 1)

            windows = pe.alloc_register("pe_windows")
            pe.reg_mov(windows, 0)

            def sum_windows(n, g):
                count = pe.value_load(group_info[0:1, bass.ds(g, 1), 1], min_val=1, max_val=nodes // WINDOW + 1)
                wait_alone(pe, messages_ready, n + 1, pe_passed)
                with pe.Fori(0, count):
                    pe.reg_add(windows, windows, 1)
                    wait_alone(pe, onehot_ready, pe.snap(windows, min_val=1, max_val=1 << 30), pe_passed)
                    for j in range(TILES):
                        last = nc.tensor.matmul(ps_window, messages[:, j, :], onehot[:, j, :],
                                                start=(j == 0), stop=(j == TILES - 1))
                    last.then_inc(window_ready, 1)

            pe.wait_ge(info_ready, 1)
            with pe.Fori(0, layers) as layer:
                wait_alone(pe, weights_in, layer * 144 + 144, pe_passed)
                embed(layer * groups, layer, 0, 0)
                with pe.Fori(0, pairs) as i:
                    n = layer * groups + i * 2
                    embed(n + 1, layer, i, 1)
                    sum_windows(n, i * 2)
                    embed(n + 2, layer, i + 1, 0)
                    sum_windows(n + 1, i * 2 + 1)
                sum_windows(layer * groups + full, full)

                wait_alone(pe, edges_done, layer + 1, pe_passed)

                def linear(r, k, wait):
                    at = pe.snap((r * CHUNK + k) * part)
                    if wait:
                        wait_alone(pe, h_copied, layer * chunks + r * CHUNK + (k - CHUNK + 1), pe_passed)
                    nc.tensor.matmul(ps_ring[k][0:feats, 0:part], w_mlp[:, :], node_sum[:, bass.ds(at, part)],
                                     start=True, stop=True).then_inc(h_ready, 1)

                for k in range(CHUNK):
                    linear(0, k, False)
                with pe.Fori(1, rounds) as r:
                    for k in range(CHUNK):
                        linear(r, k, True)

                def to_rows(r, k, wait):
                    wait_alone(pe, staged, layer * chunks + r * CHUNK + (k + 1), pe_passed)
                    if wait:
                        wait_alone(pe, rows_copied, layer * chunks + r * CHUNK + (k - CHUNK + 1), pe_passed)
                    for c in range(CHUNK):
                        last = nc.tensor.transpose(ps_ring[k][0:NODE_P, c * feats:(c + 1) * feats],
                                                   stage[:, k, c, :], ident[0:feats, 0:feats])
                    last.then_inc(rows_transposed, 1)

                for k in range(CHUNK):
                    to_rows(0, k, False)
                with pe.Fori(1, rounds) as r:
                    for k in range(CHUNK):
                        to_rows(r, k, True)

        @block.vector
        def _(dve):
            steps = dve.alloc_register("dve_steps")
            dve.reg_mov(steps, 0)

            def settle(instruction):
                instruction.then_inc(dve_step, 1)
                dve.reg_add(steps, steps, 1)
                wait_alone(dve, dve_step, dve.snap(steps, min_val=1, max_val=1 << 30), dve_passed)

            nc.vector.memset(node_sum[feats:feats + 1, :], 1.0)
            settle(nc.vector.memset(node_sum[0:feats, nodes:padded], 0.0))
            dve.wait_ge(dst_rows_in, 16 * (blocks + 1))
            for b in range(blocks + 1):
                n = min(P, full - b * P) if b < blocks else 1
                nc.vector.tensor_reduce(bounds[0:n, b, 0:1], dst_rows[0:n, b, :], AX.X, ALU.min)
                settle(nc.vector.tensor_reduce(bounds[0:n, b, 1:2], dst_rows[0:n, b, :], AX.X, ALU.max))
                settle(nc.vector.tensor_tensor(n_windows[0:n, b:b + 1], bounds[0:n, b, 1:2], bounds[0:n, b, 0:1],
                                               ALU.subtract))
                settle(nc.vector.tensor_scalar(n_windows[0:n, b:b + 1], n_windows[0:n, b:b + 1], LOG_WINDOW, None,
                                               ALU.logical_shift_right))
                settle(nc.vector.tensor_scalar(bounds[0:n, b, 1:2], n_windows[0:n, b:b + 1], 1.0, None, ALU.add))
                if b:
                    dve.wait_ge(bounds_spread, b)
                for v in range(2):
                    last = nc.vector.tensor_copy(spread_in[0:n, v, :],
                                                 bounds[0:n, b, v:v + 1].to_broadcast([n, P]))
                last.then_inc(bounds_ready, 1)
            dve.wait_ge(bounds_spread, blocks + 1)
            nc.vector.tensor_copy(base_all[:, :], ps_embed[0][:, 0:groups])
            for v in range(2):
                last = nc.vector.tensor_copy(group_info[0:1, :, v], ps_embed[v][0:1, 0:groups])
            last.then_inc(info_ready, 1)
            dve.wait_ge(info_ready, 1)
            dve.wait_ge(consts_ready, 2)

            windows = dve.alloc_register("dve_windows")
            dve.reg_mov(windows, 0)

            def group(layer, i, k, g, last_group=False):
                n = layer * groups + g
                base = dve.value_load(group_info[0:1, bass.ds(g, 1), 0], min_val=0, max_val=nodes - 1)
                count = dve.value_load(group_info[0:1, bass.ds(g, 1), 1], min_val=1, max_val=nodes // WINDOW + 1)
                wait_alone(dve, dst_in[k], slot_count(layer, i, k) * 16 + 16, dve_passed)
                settle(nc.vector.tensor_scalar(offset[:, :], dst_idx[:, k, :], base_all[:, bass.ds(g, 1)], None,
                                               ALU.subtract))
                if last_group:
                    settle(nc.vector.tensor_tensor(offset[:, :], offset[:, :], last_mask[:, :], ALU.add))
                wait_alone(dve, embedded, n + 1, dve_passed)
                for h in range(2):
                    wait_alone(dve, gather_in[k][h], slot_count(layer, i, k) * (8 * TILES) + 8 * TILES, dve_passed)
                nc.vector.tensor_tensor(summed[:, :], ps_embed[k],
                                        gathered[:, k, :, :].rearrange("p j f -> p (j f)"),
                                        ALU.add).then_inc(sum_ready, 1)
                with dve.Fori(0, count) as w:
                    nc.vector.tensor_tensor(onehot[:, :, :],
                                            window_nodes[:, :].unsqueeze(1).to_broadcast([P, TILES, WINDOW]),
                                            offset[:, :].unsqueeze(2).to_broadcast([P, TILES, WINDOW]),
                                            ALU.is_equal).then_inc(onehot_ready, 1)
                    at = nc.s_assert_within(dve.snap(base + w * WINDOW), 0, nodes - 1,
                                             skip_runtime_bounds_check_because="the last window holds a destination")
                    dve.reg_add(windows, windows, 1)
                    wait_alone(dve, window_ready, dve.snap(windows, min_val=1, max_val=1 << 30), dve_passed)
                    nc.vector.tensor_tensor(node_sum[0:feats, bass.ds(at, WINDOW)],
                                            node_sum[0:feats, bass.ds(at, WINDOW)], ps_window, ALU.add)
                    settle(nc.vector.tensor_scalar(offset[:, :], offset[:, :], float(WINDOW), None, ALU.subtract))

            with dve.Fori(0, layers) as layer:
                wait_alone(dve, node_sum_set, layer * chunks + chunks, dve_passed)
                with dve.Fori(0, pairs) as i:
                    for k in range(2):
                        group(layer, i, k, i * 2 + k)
                group(layer, pairs, 0, full, last_group=True)
                settle(nc.vector.tensor_copy(bn_tmp[0:1, 0:1], node_sum[0:1, 0:1]))
                dve.sem_inc(edges_done, 1)

                with dve.Fori(0, rounds) as r:
                    for k in range(CHUNK):
                        at = dve.snap(r * CHUNK + k)
                        nodes_at = dve.snap((r * CHUNK + k) * part)
                        wait_alone(dve, h_copied, layer * chunks + r * CHUNK + (k + 1), dve_passed)
                        nc.vector.bn_stats(stats[:, bass.ds(at, 1), :].rearrange("f o s -> f (o s)"),
                                           node_sum[0:feats, bass.ds(nodes_at, part)]).then_inc(h_counted, 1)
                wait_alone(dve, h_counted, layer * chunks + chunks, dve_passed)
                settle(nc.vector.bn_aggr(mean_var[:, :], stats[:, :, :].rearrange("f c s -> f (c s)")))
                nc.vector.tensor_scalar(bn_tmp[:, 0:1], mean_var[:, 1:2], BN_EPS, None, ALU.add).then_inc(var_ready, 1)
                wait_alone(dve, std_ready, layer + 1, dve_passed)
                settle(nc.vector.reciprocal(bn_tmp[:, 1:2], bn_tmp[:, 1:2]))
                settle(nc.vector.tensor_tensor(bn_tmp[:, 2:3], bn_tmp[:, 1:2], bn_gamma[:, :], ALU.mult))
                settle(nc.vector.tensor_tensor(bn_tmp[:, 0:1], mean_var[:, 0:1], bn_tmp[:, 2:3], ALU.mult))
                nc.vector.tensor_tensor(bn_tmp[:, 3:4], bn_beta[:, :], bn_tmp[:, 0:1],
                                        ALU.subtract).then_inc(norm_ready, 1)
                with dve.Fori(0, rounds) as r:
                    for k in range(CHUNK):
                        at = dve.snap((r * CHUNK + k) * (CHUNK * feats))
                        wait_alone(dve, rows_transposed, layer * chunks + r * CHUNK + (k + 1), dve_passed)
                        nc.vector.tensor_copy(rows[:, bass.ds(at, CHUNK * feats)],
                                              ps_ring[k][0:NODE_P, 0:CHUNK * feats]).then_inc(rows_copied, 1)

            n_cols = CHUNK * CHUNK
            width = n_cols * feats
            dve.wait_ge(x_keep_in, 16)
            dve.wait_ge(rows_copied, layers * chunks)
            dve.wait_ge(table_out, 16 * rounds * layers)
            with dve.Fori(0, rounds) as r:
                at = dve.snap(r * width)
                y = rows[:, bass.ds(at, width)]
                y3 = y.rearrange("p (c f) -> p c f", f=feats)
                settle(nc.vector.tensor_tensor(y, y, x_keep[:, bass.ds(at, width)], ALU.add))
                settle(nc.vector.tensor_reduce(ln_tmp[:, 0, :], y3, AX.X, ALU.add))
                settle(nc.vector.tensor_scalar(ln_tmp[:, 0, :], ln_tmp[:, 0, :], 1.0 / feats, None, ALU.mult))
                nc.vector.tensor_tensor(y3, y3, ln_tmp[:, 0, :].unsqueeze(2).to_broadcast([NODE_P, n_cols, feats]),
                                        ALU.subtract).then_inc(residual_ready, 1)
                wait_alone(dve, square_ready, r + 1, dve_passed)
                settle(nc.vector.tensor_reduce(ln_tmp[:, 1, :], ln_sq[:, :].rearrange("p (c f) -> p c f", f=feats),
                                               AX.X, ALU.add))
                nc.vector.tensor_scalar(ln_tmp[:, 1, :], ln_tmp[:, 1, :], 1.0 / feats, LN_EPS, ALU.mult,
                                        ALU.add).then_inc(ln_var_ready, 1)
                wait_alone(dve, ln_std_ready, r + 1, dve_passed)
                settle(nc.vector.reciprocal(ln_tmp[:, 3, :], ln_tmp[:, 2, :]))
                nc.vector.tensor_tensor(y3, y3, ln_tmp[:, 3, :].unsqueeze(2).to_broadcast([NODE_P, n_cols, feats]),
                                        ALU.mult).then_inc(ln_ready, 1)


_INS = ['x', 'src', 'dst', 'edge_attr_32', 'L0_gnn_edge_w', 'L0_gnn_edge_b', 'L0_gnn_mlp_w', 'L0_gnn_mlp_b',
        'L0_gnn_gamma', 'L0_gnn_beta']


def kernel(**inputs):
    import numpy as _np
    import concourse.bacc as _bacc
    from concourse.bass_utils import run_bass_kernel_spmd as _run

    nc = _bacc.Bacc("TRN2", target_bir_lowering=False, num_devices=1)
    arrays, args = {}, []
    for name in _INS:
        a = _np.ascontiguousarray(inputs[name])
        arrays[f"in_{name}_dram"] = a
        args.append(nc.dram_tensor(f"in_{name}_dram", a.shape, mybir.dt.from_np(a.dtype), kind="ExternalInput").ap())
    out = nc.dram_tensor("out_0_dram", inputs['x'].shape, FP32, kind="ExternalOutput").ap()
    gnn_kernel(nc, *args, out)
    return _run(nc, [arrays], core_ids=[0]).results[0]["out_0_dram"]
```

```python
import concourse.bass as bass
from concourse import mybir
from contextlib import ExitStack

FP32 = mybir.dt.float32
I32 = mybir.dt.int32
ALU = mybir.AluOpType
ACT = mybir.ActivationFunctionType
AX = mybir.AxisListType

P = 128
TILES = 8
GROUP = P * TILES
RING = 8
WINDOW = 64
LOG_WINDOW = 6
NODE_P = 100
CHUNK = 5
BANKS = 3
BACK = [next(b for b in range(1, 2 * CHUNK) if (k - b) % CHUNK % BANKS == k % BANKS)
        for k in range(CHUNK)]
MASKED = -32768.0
BN_EPS = 1e-5
LN_EPS = 1e-5
SEM_STEP = 16


def gnn_kernel(nc, x, src, dst, edge_attr, edge_w, edge_b, mlp_w, mlp_b, gamma, beta, out):
    nodes, feats = x.shape
    edges, edge_feats = edge_attr.shape
    layers = edge_w.shape[0]
    cols = nodes // NODE_P
    chunks = cols // CHUNK
    part = CHUNK * NODE_P
    rounds = chunks // CHUNK
    round_cols = CHUNK * CHUNK
    round_width = round_cols * feats
    full = edges // GROUP
    groups = full + 1
    trips = groups // RING
    tail = groups % RING
    last_edge0 = edges - GROUP
    overlap = full * GROUP - last_edge0
    blocks = -(-full // P)
    half = TILES // 2
    weight_loads = half + 3
    assert nodes == NODE_P * CHUNK * CHUNK * rounds and half * edge_feats == P and 0 <= overlap < GROUP
    assert 0 < full - (blocks - 1) * P < P and tail
    padded = nodes + WINDOW

    table = nc.dram_tensor("node_table", (nodes, feats), FP32, kind="Internal").ap()
    x_rows = x.rearrange("(p c) f -> p (c f)", p=NODE_P)
    table_rows = table.rearrange("(p c) f -> p (c f)", p=NODE_P)
    out_rows = out.rearrange("(p c) f -> p (c f)", p=NODE_P)
    src_groups = src[0:full * GROUP].rearrange("(g p j) -> p g j", p=P, j=TILES)
    dst_groups = dst[0:full * GROUP].rearrange("(g p j) -> p g j", p=P, j=TILES)
    attr_groups = edge_attr[0:full * GROUP, :].rearrange("(g p j) f -> p g (j f)", p=P, j=TILES)
    src_last = src[last_edge0:edges].rearrange("(p j) -> p j", p=P)
    dst_last = dst[last_edge0:edges].rearrange("(p j) -> p j", p=P)
    attr_last = edge_attr[last_edge0:edges, :].rearrange("(p j) f -> p (j f)", p=P)

    ctx = ExitStack()
    with ctx:
        def sb(name, shape, dt=FP32):
            return ctx.enter_context(nc.sbuf_tensor(name, shape, dt))

        def sem(name):
            return ctx.enter_context(nc.semaphore(name))

        node_h = sb("node_h", [feats + 1, padded])
        rows = sb("rows", [NODE_P, cols * feats])
        x_keep = sb("x_keep", [NODE_P, cols * feats])
        ident = sb("ident", [P, P])
        centre = sb("centre", [feats, feats])
        iota_nodes = sb("iota_nodes", [P, WINDOW])
        last_mask = sb("last_mask", [P, TILES])
        ones_row = sb("ones_row", [1, P])
        table_load = sb("table_load", [1, 1])
        base_all = sb("base_all", [P, groups])
        group_info = sb("group_info", [1, groups, 2], I32)
        bn_gamma = sb("bn_gamma", [feats, layers])
        bn_beta = sb("bn_beta", [feats, layers])
        w_edge = sb("w_edge", [P, half * feats])
        b_edge = sb("b_edge", [P, feats])
        w_mlp = sb("w_mlp", [feats + 1, feats])
        src_idx = sb("src_idx", [P, RING, TILES], I32)
        dst_idx = sb("dst_idx", [P, RING, TILES], I32)
        attr = sb("attr", [P, RING, TILES * edge_feats])
        gathered = sb("gathered", [P, RING, TILES, feats])
        attr_t = sb("attr_t", [P, 2 * P])
        summed = sb("summed", [P, TILES * feats])
        messages = sb("messages", [P, TILES, feats])
        offset = sb("offset", [P, 2, TILES])
        onehot = sb("onehot", [P, 2, TILES, WINDOW])
        window_sum = sb("window_sum", [feats, WINDOW])
        stage = sb("stage", [feats + 1, CHUNK, CHUNK, NODE_P])
        stats = sb("stats", [feats, chunks, 6])
        mean_var = sb("mean_var", [feats, 2])
        bn_tmp = sb("bn_tmp", [feats, 4])
        dst_rows = sb("dst_rows", [P, blocks + 1, GROUP], I32)
        bounds = sb("bounds", [P, blocks + 1, 2])
        n_windows = sb("n_windows", [P, blocks + 1], I32)
        spread_in = sb("spread_in", [P, blocks + 1, 2, P])
        x_in = sb("x_in", [NODE_P, CHUNK, CHUNK * feats])
        x_mean = sb("x_mean", [NODE_P, cols])
        ln_sq = sb("ln_sq", [NODE_P, CHUNK, CHUNK * feats])
        ln_var = sb("ln_var", [NODE_P, cols])
        ln_std = sb("ln_std", [NODE_P, cols])

        ps = ctx.enter_context(nc.psum_tensor("ps", [P, 8, 512], FP32))
        ps_embed = [ps[:, 0, :], ps[:, 1, :]]
        ps_attr = ps[:, 2, 0:2 * P]
        ps_window = ps[0:feats, 3, 0:WINDOW]
        ps_mapped = ps[0:feats, 4, 0:WINDOW]
        window_nodes = ps[:, 7, 0:WINDOW]
        ps_map = [ps[0:feats, k, 0:part] for k in range(BANKS)]
        ps_turn = [ps[:, 4 + k, :] for k in range(BANKS)]
        ps_base = ps[:, 3, 0:groups]
        ps_windows = ps[:, 7, WINDOW:WINDOW + groups]

        dst_rows_in = sem("dst_rows_in")
        x_in_in = [sem(f"x_in_in{k}") for k in range(CHUNK)]
        x_keep_in = sem("x_keep_in")
        norm_weights_in = sem("norm_weights_in")
        weights_in = sem("weights_in")
        src_in = [sem(f"src_in{k}") for k in range(RING)]
        dst_in = [sem(f"dst_in{k}") for k in range(RING)]
        attr_in = [sem(f"attr_in{k}") for k in range(RING)]
        gather_in = [sem(f"gather_in{k}") for k in range(RING)]
        table_out = sem("table_out")
        result_out = sem("result_out")
        consts_ready = sem("consts_ready")
        ones_ready = sem("ones_ready")
        stage_ones_ready = sem("stage_ones_ready")
        x_transposed = sem("x_transposed")
        x_staged = sem("x_staged")
        x_mapped = sem("x_mapped")
        x_map_copied = sem("x_map_copied")
        bounds_ready = sem("bounds_ready")
        bounds_spread = sem("bounds_spread")
        info_ready = sem("info_ready")
        attr_transposed = sem("attr_transposed")
        attr_t_ready = sem("attr_t_ready")
        embedded = sem("embedded")
        bias_added = sem("bias_added")
        sum_ready = sem("sum_ready")
        messages_ready = sem("messages_ready")
        first_onehot_ready = sem("first_onehot_ready")
        more_onehot_ready = sem("more_onehot_ready")
        window_ready = sem("window_ready")
        window_copied = sem("window_copied")
        window_mapped = sem("window_mapped")
        edges_done = sem("edges_done")
        chunks_counted = sem("chunks_counted")
        var_ready = sem("var_ready")
        std_ready = sem("std_ready")
        norm_ready = sem("norm_ready")
        staged = sem("staged")
        rows_transposed = sem("rows_transposed")
        rows_copied = sem("rows_copied")
        input_ready = sem("input_ready")
        squares_added = sem("squares_added")
        node_ones_ready = sem("node_ones_ready")
        mapped = sem("mapped")
        map_copied = sem("map_copied")
        square_ready = sem("square_ready")
        ln_var_ready = sem("ln_var_ready")
        ln_std_ready = sem("ln_std_ready")
        ln_scale_ready = sem("ln_scale_ready")
        ln_ready = sem("ln_ready")
        dve_step = sem("dve_step")
        pool_step = sem("pool_step")
        sp_passed = sem("sp_passed")
        pool_passed = sem("pool_passed")
        act_passed = sem("act_passed")
        pe_passed = sem("pe_passed")
        dve_passed = sem("dve_passed")

        block = ctx.enter_context(nc.Block())

        def wait_alone(eng, s, value, passed):
            eng.wait_ge(s, value)
            eng.sem_inc(passed, 1)

        def one_ahead(eng, first, second, before_last_round=None):
            first(0, 0)
            for k in range(CHUNK):
                first(k // (CHUNK - 1), (k + 1) % CHUNK)
                second(0, k)
            with eng.Fori(1, rounds - 1) as r:
                for k in range(CHUNK):
                    first(r + k // (CHUNK - 1), (k + 1) % CHUNK)
                    second(r, k)
            if before_last_round:
                before_last_round()
            for k in range(CHUNK):
                if k < CHUNK - 1:
                    first(rounds - 1, k + 1)
                second(rounds - 1, k)

        def reused(r, k, slots):
            return not isinstance(r, int) or r > 0 or k >= slots

        def slot_count(layer, i, k):
            return layer * (trips + (k < tail)) + i

        by_column = node_h[0:feats, 0:nodes].rearrange("f (p c) -> f c p", c=cols)

        @block.sync
        def _(sp):
            def load_weights(layer):
                w = edge_w[bass.ds(layer, 1), :, :].rearrange("o k f -> (o k) f")
                for q in range(half):
                    sp.dma_start(w_edge[q * edge_feats:(q + 1) * edge_feats, q * feats:(q + 1) * feats],
                                 w).then_inc(weights_in, SEM_STEP)
                sp.dma_start(b_edge[:, :], edge_b[bass.ds(layer, 1), :].to_broadcast([P, feats])).then_inc(weights_in, SEM_STEP)
                sp.dma_start(w_mlp[0:feats, :], mlp_w[bass.ds(layer, 1), :, :].rearrange("o k f -> (o k) f")
                             ).then_inc(weights_in, SEM_STEP)
                sp.dma_start(w_mlp[feats:feats + 1, :], mlp_b[bass.ds(layer, 1), :]).then_inc(weights_in, SEM_STEP)

            def load_group(k, s, d, a):
                sp.dma_start(src_idx[:, k, :], s).then_inc(src_in[k], SEM_STEP)
                sp.dma_start(dst_idx[:, k, :], d).then_inc(dst_in[k], SEM_STEP)
                sp.dma_start(attr[:, k, :], a).then_inc(attr_in[k], SEM_STEP)

            def group_of(view, g):
                return view[:, bass.ds(g, 1), :].rearrange("p o n -> p (o n)")

            def wait_slot(layer, i, k):
                wait_alone(sp, gather_in[k], slot_count(layer, i, k) * (SEM_STEP * TILES), sp_passed)
                wait_alone(sp, attr_transposed, layer * groups + i * RING + (k - RING + 1), sp_passed)
                wait_alone(sp, sum_ready, layer * groups + i * RING + (k - RING + 1), sp_passed)

            def first_groups(some):
                for k in some:
                    load_group(k, src_groups[:, k, :], dst_groups[:, k, :], attr_groups[:, k, :])

            def later_groups(layer):
                with sp.Fori(1, trips) as i:
                    for k in range(RING):
                        g = sp.snap(i * RING + k)
                        wait_slot(layer, i, k)
                        load_group(k, group_of(src_groups, g), group_of(dst_groups, g), group_of(attr_groups, g))
                for k in range(tail):
                    g = trips * RING + k
                    wait_slot(layer, trips, k)
                    if g < full:
                        load_group(k, src_groups[:, g, :], dst_groups[:, g, :], attr_groups[:, g, :])
                    else:
                        load_group(k, src_last, dst_last, attr_last)

            first_groups([0])
            step = CHUNK * feats
            for k in range(CHUNK):
                sp.dma_start(x_in[:, k, :], x_rows[:, k * step:(k + 1) * step]).then_inc(x_in_in[k], SEM_STEP)
            sp.wait_ge(consts_ready, 1)
            load_weights(0)
            first_groups([1])
            for b in range(blocks):
                n = min(P, full - b * P)
                sp.dma_start(dst_rows[0:n, b, :],
                             dst[b * P * GROUP:(b * P + n) * GROUP].rearrange("(g e) -> g e", e=GROUP)
                             ).then_inc(dst_rows_in, SEM_STEP)
            sp.dma_start(dst_rows[0:1, blocks, :],
                         dst[last_edge0:edges].rearrange("(o e) -> o e", o=1)).then_inc(dst_rows_in, SEM_STEP)
            first_groups(range(2, RING))
            with sp.Fori(1, rounds) as r:
                for k in range(CHUNK):
                    at = sp.snap((r * CHUNK + k) * step)
                    wait_alone(sp, x_transposed, r * CHUNK + (k - CHUNK + 1), sp_passed)
                    sp.dma_start(x_in[:, k, :], x_rows[:, bass.ds(at, step)]).then_inc(x_in_in[k], SEM_STEP)
            sp.dma_start(bn_gamma[:, :], gamma.rearrange("l f -> f l"),
                         allow_slow_non_contiguous=True).then_inc(norm_weights_in, SEM_STEP)
            sp.dma_start(bn_beta[:, :], beta.rearrange("l f -> f l"),
                         allow_slow_non_contiguous=True).then_inc(norm_weights_in, SEM_STEP)
            sp.dma_start(x_keep[:, :], x_rows).then_inc(x_keep_in, SEM_STEP)

            with sp.Fori(0, layers - 1) as layer:
                later_groups(layer)
                wait_alone(sp, edges_done, layer + 1, sp_passed)
                first_groups(range(RING))
                load_weights(layer + 1)
                with sp.Fori(0, rounds) as r:
                    at = sp.snap(r * round_width)
                    wait_alone(sp, rows_copied, layer * chunks + r * CHUNK + CHUNK, sp_passed)
                    sp.dma_start(table_rows[:, bass.ds(at, round_width)],
                                 rows[:, bass.ds(at, round_width)]).then_inc(table_out, SEM_STEP)
            later_groups(layers - 1)

            with sp.Fori(0, rounds) as r:
                at = sp.snap(r * round_width)
                wait_alone(sp, ln_ready, r + 1, sp_passed)
                sp.dma_start(out_rows[:, bass.ds(at, round_width)],
                             rows[:, bass.ds(at, round_width)]).then_inc(result_out, SEM_STEP)
            sp.wait_ge(table_out, SEM_STEP * rounds * (layers - 1))
            sp.wait_ge(result_out, SEM_STEP * rounds)

        @block.gpsimd
        def _(pool):
            nc.gpsimd.memset(w_edge[:, :], 0.0).then_inc(consts_ready, 1)
            nc.gpsimd.memset(ones_row[:, :], 1.0).then_inc(ones_ready, 1)
            nc.gpsimd.memset(last_mask[:, :], 0.0)
            nc.gpsimd.memset(centre[:, :], -1.0 / feats)
            nc.gpsimd.iota(iota_nodes[:, :], [[1, WINDOW]], base=0, channel_multiplier=0,
                           allow_small_or_imprecise_dtypes=True)
            nc.gpsimd.memset(ident[:, :], 0.0).then_inc(pool_step, 1)
            pool.wait_ge(pool_step, 1)
            nc.gpsimd.affine_select(out=ident[:, :], in_=ident[:, :], pattern=[[-1, P]],
                                    compare_op=ALU.not_equal, fill=1.0, base=0, channel_multiplier=1)
            nc.gpsimd.affine_select(out=centre[:, :], in_=centre[:, :], pattern=[[-1, feats]],
                                    compare_op=ALU.not_equal, fill=1.0 - 1.0 / feats, base=0, channel_multiplier=1)
            nc.gpsimd.affine_select(out=last_mask[:, :], in_=last_mask[:, :], pattern=[[1, TILES]],
                                    compare_op=ALU.is_ge, fill=MASKED, base=-overlap,
                                    channel_multiplier=TILES).then_inc(consts_ready, 1)

            last_node = pool.to_reg(nodes - 1)

            def gather_group(features, layer, i, k, wait):
                wait_alone(pool, src_in[k], slot_count(layer, i, k) * SEM_STEP + SEM_STEP, pool_passed)
                if wait:
                    wait_alone(pool, sum_ready, layer * groups + i * RING + (k - RING + 1), pool_passed)
                for j in range(TILES):
                    pool.indirect_dma_start(
                        out=gathered[:, k, j, :], out_offset=None, in_=features,
                        in_offset=bass.IndirectOffsetOnAxis(ap=src_idx[:, k, j:j + 1], axis=0),
                        bounds_check=last_node).then_inc(gather_in[k], SEM_STEP)

            def layer_gathers(layer, features):
                for k in range(RING):
                    gather_group(features, layer, 0, k, False)
                with pool.Fori(1, trips) as i:
                    for k in range(RING):
                        gather_group(features, layer, i, k, True)
                for k in range(tail):
                    gather_group(features, layer, trips, k, True)

            layer_gathers(0, x[:, :])
            with pool.Fori(1, layers) as layer:
                wait_alone(pool, table_out, layer * (SEM_STEP * rounds), pool_passed)
                layer_gathers(layer, table[:, :])

            with pool.Fori(0, rounds - 1) as r:
                at = pool.snap(r * round_width)
                at_col = pool.snap(r * round_cols)
                wait_alone(pool, ln_scale_ready, r + 1, pool_passed)
                y = rows[:, bass.ds(at, round_width)].rearrange("p (c f) -> p c f", f=feats)
                scale = ln_std[:, bass.ds(at_col, round_cols)].unsqueeze(2).to_broadcast([NODE_P, round_cols, feats])
                nc.gpsimd.tensor_tensor(y, y, scale, ALU.mult).then_inc(ln_ready, 1)

        @block.scalar
        def _(act):
            def stage_x(r, k):
                wait_alone(act, x_transposed, r * CHUNK + (k + 1), act_passed)
                if reused(r, k, CHUNK):
                    wait_alone(act, x_mapped, r * CHUNK + (k - CHUNK + 1), act_passed)
                nc.scalar.copy(stage[0:feats, k, :, :].rearrange("f c p -> f (c p)"),
                               ps_turn[k % BANKS][0:feats, 0:part]).then_inc(x_staged, 1)

            def copy_x_map(r, k):
                at = act.snap((r * CHUNK + k) * CHUNK)
                wait_alone(act, x_mapped, r * CHUNK + (k + 1), act_passed)
                nc.scalar.copy(by_column[:, bass.ds(at, CHUNK), :],
                               ps_map[k % BANKS].rearrange("f (c p) -> f c p", c=CHUNK)).then_inc(x_map_copied, 1)

            def copy_attr(n):
                wait_alone(act, attr_transposed, n + 1, act_passed)
                nc.scalar.copy(attr_t[:, :], ps_attr).then_inc(attr_t_ready, 1)

            def relu_messages(n):
                wait_alone(act, sum_ready, n + 1, act_passed)
                nc.scalar.activation(messages[:, :, :].rearrange("p j f -> p (j f)"), summed[:, :],
                                     ACT.Relu).then_inc(messages_ready, 1)

            def edge_phase(layer):
                copy_attr(layer * groups)
                with act.Fori(0, trips) as i:
                    for k in range(RING):
                        n = layer * groups + i * RING + k
                        copy_attr(n + 1)
                        relu_messages(n)
                for k in range(tail):
                    n = layer * groups + trips * RING + k
                    if k < tail - 1:
                        copy_attr(n + 1)
                    relu_messages(n)

            def normalise(layer, r, k):
                at = act.snap((r * CHUNK + k) * CHUNK)
                if reused(r, k, CHUNK):
                    wait_alone(act, rows_transposed, layer * chunks + r * CHUNK + (k - CHUNK + 1), act_passed)
                nc.scalar.activation(stage[0:feats, k, :, :], by_column[:, bass.ds(at, CHUNK), :], ACT.Relu,
                                     bias=bn_tmp[:, 3:4], scale=bn_tmp[:, 2:3]).then_inc(staged, 1)

            def normalise_in_place(r, k):
                at = act.snap((r * CHUNK + k) * part)
                nc.scalar.activation(node_h[0:feats, bass.ds(at, part)], node_h[0:feats, bass.ds(at, part)],
                                     ACT.Relu, bias=bn_tmp[:, 3:4], scale=bn_tmp[:, 2:3]).then_inc(input_ready, 1)

            def square(r, k):
                at = act.snap((r * CHUNK + k) * (CHUNK * feats))
                wait_alone(act, rows_copied, (layers - 1) * chunks + r * CHUNK + (k + 1), act_passed)
                nc.scalar.activation(ln_sq[:, k, :], rows[:, bass.ds(at, CHUNK * feats)],
                                     ACT.Square).then_inc(square_ready, 1)

            def batch_scale(layer):
                wait_alone(act, var_ready, layer + 1, act_passed)
                nc.scalar.activation(bn_tmp[:, 1:2], bn_tmp[:, 0:1], ACT.Sqrt).then_inc(std_ready, 1)
                wait_alone(act, norm_ready, layer + 1, act_passed)

            def layer_norm_std(r):
                at = act.snap(r * round_cols)
                wait_alone(act, ln_var_ready, r + 1, act_passed)
                nc.scalar.activation(ln_std[:, bass.ds(at, round_cols)], ln_var[:, bass.ds(at, round_cols)],
                                     ACT.Sqrt).then_inc(ln_std_ready, 1)

            act.wait_ge(ones_ready, 1)
            nc.scalar.activation(table_load[:, :], ones_row[:, 0:1], ACT.Sqrt)
            one_ahead(act, stage_x, copy_x_map)

            with act.Fori(0, layers - 1) as layer:
                edge_phase(layer)
                batch_scale(layer)
                for k in range(CHUNK):
                    normalise(layer, 0, k)
                with act.Fori(1, rounds) as r:
                    for k in range(CHUNK):
                        normalise(layer, r, k)

                def copy_map(r, k):
                    at = act.snap((r * CHUNK + k) * part)
                    wait_alone(act, mapped, layer * chunks + r * CHUNK + (k + 1), act_passed)
                    nc.scalar.copy(node_h[0:feats, bass.ds(at, part)], ps_map[k % BANKS]).then_inc(map_copied, 1)

                wait_alone(act, staged, layer * chunks + chunks, act_passed)
                one_ahead(act, normalise_in_place, copy_map)

            edge_phase(layers - 1)
            batch_scale(layers - 1)
            for k in range(CHUNK):
                normalise(layers - 1, 0, k)
            for k in range(CHUNK):
                square(0, k)
                normalise(layers - 1, 1, k)
            with act.Fori(2, rounds) as r:
                for k in range(CHUNK):
                    square(r - 1, k)
                    normalise(layers - 1, r, k)
                    if k == CHUNK // 2:
                        layer_norm_std(r - 2)
            layer_norm_std(rounds - 2)
            for k in range(CHUNK):
                square(rounds - 1, k)
            layer_norm_std(rounds - 1)

        @block.tensor
        def _(pe):
            pe.wait_ge(consts_ready, 2)

            def transpose_x(r, k):
                wait_alone(pe, x_in_in[k], r * SEM_STEP + SEM_STEP, pe_passed)
                if reused(r, k, BANKS):
                    wait_alone(pe, x_staged, r * CHUNK + (k - BACK[k] + 1), pe_passed)
                for c in range(CHUNK):
                    last = nc.tensor.transpose(ps_turn[k % BANKS][0:feats, c * NODE_P:(c + 1) * NODE_P],
                                               x_in[:, k, c * feats:(c + 1) * feats],
                                               ident[0:NODE_P, 0:NODE_P])
                last.then_inc(x_transposed, 1)

            def map_x(r, k):
                wait_alone(pe, x_staged, r * CHUNK + (k + 1), pe_passed)
                if reused(r, k, BANKS):
                    wait_alone(pe, x_map_copied, r * CHUNK + (k - BACK[k] + 1), pe_passed)
                elif k == 0:
                    pe.wait_ge(weights_in, SEM_STEP * weight_loads)
                    pe.wait_ge(stage_ones_ready, 1)
                nc.tensor.matmul(ps_map[k % BANKS], w_mlp[:, :],
                                 stage[:, k, :, :].rearrange("f c p -> f (c p)"),
                                 start=True, stop=True).then_inc(x_mapped, 1)

            def spread_bounds():
                for b in range(blocks + 1):
                    n = min(P, full - b * P) if b < blocks else 1
                    at = b * P if b < blocks else full
                    pe.wait_ge(bounds_ready, b + 1)
                    nc.tensor.matmul(ps_base[:, at:at + n], spread_in[0:n, b, 0, :], ident[0:n, 0:n],
                                     start=True, stop=True)
                    nc.tensor.matmul(ps_windows[:, at:at + n], spread_in[0:n, b, 1, :], ident[0:n, 0:n],
                                     start=True, stop=True).then_inc(bounds_spread, 1)

            one_ahead(pe, transpose_x, map_x, spread_bounds)

            def embed(n, layer, i, k):
                wait_alone(pe, attr_in[k], slot_count(layer, i, k) * SEM_STEP + SEM_STEP, pe_passed)
                for q in range(2):
                    last = nc.tensor.transpose(ps_attr[:, q * P:(q + 1) * P], attr[:, k, q * P:(q + 1) * P],
                                               ident[:, :])
                last.then_inc(attr_transposed, 1)
                wait_alone(pe, attr_t_ready, n + 1, pe_passed)
                width = half * feats
                for q in range(2):
                    last = nc.tensor.matmul(ps_embed[k % 2][:, q * width:(q + 1) * width],
                                            attr_t[:, q * P:(q + 1) * P], w_edge[:, :], start=True, stop=True)
                last.then_inc(embedded, 1)

            windows = pe.alloc_register("pe_windows")
            pe.reg_mov(windows, 0)
            more_windows = pe.alloc_register("pe_more_windows")
            pe.reg_mov(more_windows, 0)

            def sum_window(k):
                pe.reg_add(windows, windows, 1)
                windows_now = pe.snap(windows, min_val=1, max_val=1 << 30)
                for j in range(TILES):
                    last = nc.tensor.matmul(ps_window, messages[:, j, :], onehot[:, k % 2, j, :],
                                            start=(j == 0), stop=(j == TILES - 1))
                last.then_inc(window_ready, 1)
                wait_alone(pe, window_copied, windows_now, pe_passed)
                nc.tensor.matmul(ps_mapped, w_mlp[0:feats, :], window_sum[:, :],
                                 start=True, stop=True).then_inc(window_mapped, 1)

            def sum_windows(n, k, g):
                count = pe.value_load(group_info[0:1, bass.ds(g, 1), 1], min_val=1, max_val=nodes // WINDOW + 1)
                wait_alone(pe, first_onehot_ready, n + 1, pe_passed)
                wait_alone(pe, messages_ready, n + 1, pe_passed)
                sum_window(k)
                with pe.If(count > 1), pe.Fori(1, count):
                    pe.reg_add(more_windows, more_windows, 1)
                    wait_alone(pe, more_onehot_ready, pe.snap(more_windows, min_val=1, max_val=1 << 30), pe_passed)
                    sum_window(k)

            def edge_phase(layer):
                wait_alone(pe, weights_in, layer * (SEM_STEP * weight_loads) + SEM_STEP * weight_loads, pe_passed)
                embed(layer * groups, layer, 0, 0)
                with pe.Fori(0, trips) as i:
                    for k in range(RING):
                        n = layer * groups + i * RING + k
                        if k < RING - 1:
                            embed(n + 1, layer, i, k + 1)
                        else:
                            embed(n + 1, layer, i + 1, 0)
                        sum_windows(n, k, i * RING + k)
                for k in range(tail):
                    n = layer * groups + trips * RING + k
                    if k < tail - 1:
                        embed(n + 1, layer, trips, k + 1)
                    sum_windows(n, k, trips * RING + k)
                wait_alone(pe, edges_done, layer + 1, pe_passed)

            def to_rows(layer, r, k, turn):
                wait_alone(pe, staged, layer * chunks + r * CHUNK + (k + 1), pe_passed)
                if reused(r, k, BANKS):
                    wait_alone(pe, rows_copied, layer * chunks + r * CHUNK + (k - BACK[k] + 1), pe_passed)
                for c in range(CHUNK):
                    last = turn(ps_turn[k % BANKS][0:NODE_P, c * feats:(c + 1) * feats], stage[0:feats, k, c, :])
                last.then_inc(rows_transposed, 1)

            def node_phase(layer, turn):
                for k in range(CHUNK):
                    to_rows(layer, 0, k, turn)
                with pe.Fori(1, rounds) as r:
                    for k in range(CHUNK):
                        to_rows(layer, r, k, turn)

            def transpose_chunk(to, nodes_t):
                return nc.tensor.transpose(to, nodes_t, ident[0:feats, 0:feats])

            def centre_chunk(to, nodes_t):
                return nc.tensor.matmul(to, nodes_t, centre[:, :], start=True, stop=True)

            def map_nodes(layer, r, k):
                at = pe.snap((r * CHUNK + k) * part)
                wait_alone(pe, input_ready, layer * chunks + r * CHUNK + (k + 1), pe_passed)
                if reused(r, k, BANKS):
                    wait_alone(pe, map_copied, layer * chunks + r * CHUNK + (k - BACK[k] + 1), pe_passed)
                nc.tensor.matmul(ps_map[k % BANKS], w_mlp[:, :], node_h[:, bass.ds(at, part)],
                                 start=True, stop=True).then_inc(mapped, 1)

            pe.wait_ge(info_ready, 1)
            pe.wait_ge(node_ones_ready, 1)
            pe.wait_ge(x_map_copied, chunks)
            with pe.Fori(0, layers - 1) as layer:
                edge_phase(layer)
                node_phase(layer, transpose_chunk)
                wait_alone(pe, weights_in, (layer + 1) * (SEM_STEP * weight_loads) + SEM_STEP * weight_loads,
                           pe_passed)
                for k in range(CHUNK):
                    map_nodes(layer, 0, k)
                with pe.Fori(1, rounds) as r:
                    for k in range(CHUNK):
                        map_nodes(layer, r, k)
                wait_alone(pe, map_copied, layer * chunks + chunks, pe_passed)
            edge_phase(layers - 1)
            node_phase(layers - 1, centre_chunk)

        @block.vector
        def _(dve):
            steps = dve.alloc_register("dve_steps")
            dve.reg_mov(steps, 0)

            def settle(instruction):
                instruction.then_inc(dve_step, 1)
                dve.reg_add(steps, steps, 1)
                wait_alone(dve, dve_step, dve.snap(steps, min_val=1, max_val=1 << 30), dve_passed)

            nc.vector.memset(stage[feats:feats + 1, :, :, :].rearrange("o k c p -> o (k c p)"), 1.0
                             ).then_inc(stage_ones_ready, 1)
            nc.vector.memset(node_h[0:feats, nodes:padded], 0.0)
            dve.wait_ge(consts_ready, 2)
            nc.vector.tensor_copy(window_nodes, iota_nodes[:, :])
            dve.wait_ge(dst_rows_in, SEM_STEP * (blocks + 1))
            for b in range(blocks + 1):
                n = min(P, full - b * P) if b < blocks else 1
                nc.vector.tensor_reduce(bounds[0:n, b, 0:1], dst_rows[0:n, b, :], AX.X, ALU.min)
                settle(nc.vector.tensor_reduce(bounds[0:n, b, 1:2], dst_rows[0:n, b, :], AX.X, ALU.max))
                settle(nc.vector.tensor_tensor(n_windows[0:n, b:b + 1], bounds[0:n, b, 1:2], bounds[0:n, b, 0:1],
                                               ALU.subtract))
                settle(nc.vector.tensor_scalar(n_windows[0:n, b:b + 1], n_windows[0:n, b:b + 1], LOG_WINDOW, None,
                                               ALU.logical_shift_right))
                settle(nc.vector.tensor_scalar(bounds[0:n, b, 1:2], n_windows[0:n, b:b + 1], 1.0, None, ALU.add))
                for v in range(2):
                    last = nc.vector.tensor_copy(spread_in[0:n, b, v, :],
                                                 bounds[0:n, b, v:v + 1].to_broadcast([n, P]))
                last.then_inc(bounds_ready, 1)

            nc.vector.memset(node_h[feats:feats + 1, :], 1.0).then_inc(node_ones_ready, 1)
            dve.wait_ge(bounds_spread, blocks + 1)
            nc.vector.tensor_copy(base_all[:, :], ps_base)
            nc.vector.tensor_copy(group_info[0:1, :, 0], ps_base[0:1, :])
            nc.vector.tensor_copy(group_info[0:1, :, 1], ps_windows[0:1, :]).then_inc(info_ready, 1)
            dve.wait_ge(info_ready, 1)

            windows = dve.alloc_register("dve_windows")
            dve.reg_mov(windows, 0)

            def make_onehot(k):
                return nc.vector.tensor_tensor(onehot[:, k % 2, :, :],
                                               window_nodes.unsqueeze(1).to_broadcast([P, TILES, WINDOW]),
                                               offset[:, k % 2, :].unsqueeze(2).to_broadcast([P, TILES, WINDOW]),
                                               ALU.is_equal)

            def prepare(layer, i, k, g, last_group=False):
                wait_alone(dve, dst_in[k], slot_count(layer, i, k) * SEM_STEP + SEM_STEP, dve_passed)
                settle(nc.vector.tensor_scalar(offset[:, k % 2, :], dst_idx[:, k, :], base_all[:, bass.ds(g, 1)], None,
                                               ALU.subtract))
                if last_group:
                    settle(nc.vector.tensor_tensor(offset[:, k % 2, :], offset[:, k % 2, :], last_mask[:, :], ALU.add))
                make_onehot(k).then_inc(first_onehot_ready, 1)
                wait_alone(dve, embedded, layer * groups + g + 1, dve_passed)
                embeddings = ps_embed[k % 2].rearrange("p (j f) -> p j f", f=feats)
                nc.vector.tensor_tensor(embeddings, embeddings,
                                        b_edge[:, :].unsqueeze(1).to_broadcast([P, TILES, feats]),
                                        ALU.add).then_inc(bias_added, 1)

            def add_window(at):
                dve.reg_add(windows, windows, 1)
                windows_now = dve.snap(windows, min_val=1, max_val=1 << 30)
                wait_alone(dve, window_ready, windows_now, dve_passed)
                nc.vector.tensor_copy(window_sum[:, :], ps_window).then_inc(window_copied, 1)
                wait_alone(dve, window_mapped, windows_now, dve_passed)
                settle(nc.vector.tensor_tensor(node_h[0:feats, bass.ds(at, WINDOW)],
                                               node_h[0:feats, bass.ds(at, WINDOW)], ps_mapped, ALU.add))

            def group(layer, i, k, g, prepare_next=None):
                n = layer * groups + g
                wait_alone(dve, bias_added, n + 1, dve_passed)
                wait_alone(dve, gather_in[k],
                           slot_count(layer, i, k) * (SEM_STEP * TILES) + SEM_STEP * TILES, dve_passed)
                nc.vector.tensor_tensor(summed[:, :], ps_embed[k % 2],
                                        gathered[:, k, :, :].rearrange("p j f -> p (j f)"),
                                        ALU.add).then_inc(sum_ready, 1)
                if prepare_next:
                    prepare_next()
                base = dve.value_load(group_info[0:1, bass.ds(g, 1), 0], min_val=0, max_val=nodes - 1)
                count = dve.value_load(group_info[0:1, bass.ds(g, 1), 1], min_val=1, max_val=nodes // WINDOW + 1)
                add_window(base)
                with dve.If(count > 1), dve.Fori(1, count) as w:
                    settle(nc.vector.tensor_scalar(offset[:, k % 2, :], offset[:, k % 2, :], float(WINDOW), None,
                                                   ALU.subtract))
                    make_onehot(k).then_inc(more_onehot_ready, 1)
                    add_window(nc.s_assert_within(
                        dve.snap(base + w * WINDOW), 0, nodes - 1,
                        skip_runtime_bounds_check_because="the last window holds a destination"))

            def edge_phase(layer):
                prepare(layer, 0, 0, 0)
                with dve.Fori(0, trips) as i:
                    for k in range(RING):
                        j, next_k = (i, k + 1) if k < RING - 1 else (i + 1, 0)
                        group(layer, i, k, i * RING + k, lambda: prepare(layer, j, next_k, i * RING + (k + 1)))
                for k in range(tail):
                    g = trips * RING + k
                    if k < tail - 1:
                        group(layer, trips, k, g,
                              lambda: prepare(layer, trips, k + 1, g + 1, last_group=(k == tail - 2)))
                    else:
                        group(layer, trips, k, g)
                dve.sem_inc(edges_done, 1)

            def batch_norm(layer):
                with dve.Fori(0, rounds) as r:
                    for k in range(CHUNK):
                        m = dve.snap(r * CHUNK + k)
                        at = dve.snap((r * CHUNK + k) * part)
                        nc.vector.bn_stats(stats[:, bass.ds(m, 1), :].rearrange("f o s -> f (o s)"),
                                           node_h[0:feats, bass.ds(at, part)]).then_inc(chunks_counted, 1)
                wait_alone(dve, chunks_counted, layer * chunks + chunks, dve_passed)
                settle(nc.vector.bn_aggr(mean_var[:, :], stats[:, :, :].rearrange("f c s -> f (c s)")))
                nc.vector.tensor_scalar(bn_tmp[:, 0:1], mean_var[:, 1:2], BN_EPS, None, ALU.add).then_inc(var_ready, 1)
                wait_alone(dve, std_ready, layer + 1, dve_passed)
                settle(nc.vector.reciprocal(bn_tmp[:, 1:2], bn_tmp[:, 1:2]))
                settle(nc.vector.tensor_tensor(bn_tmp[:, 2:3], bn_tmp[:, 1:2], bn_gamma[:, bass.ds(layer, 1)],
                                               ALU.mult))
                settle(nc.vector.tensor_tensor(bn_tmp[:, 0:1], mean_var[:, 0:1], bn_tmp[:, 2:3], ALU.mult))
                nc.vector.tensor_tensor(bn_tmp[:, 3:4], bn_beta[:, bass.ds(layer, 1)], bn_tmp[:, 0:1],
                                        ALU.subtract).then_inc(norm_ready, 1)

            dve.wait_ge(norm_weights_in, 2 * SEM_STEP)
            dve.wait_ge(x_map_copied, chunks)
            with dve.Fori(0, layers - 1) as layer:
                edge_phase(layer)
                batch_norm(layer)
                with dve.Fori(0, rounds) as r:
                    for k in range(CHUNK):
                        at = dve.snap((r * CHUNK + k) * (CHUNK * feats))
                        wait_alone(dve, rows_transposed, layer * chunks + r * CHUNK + (k + 1), dve_passed)
                        nc.vector.tensor_copy(rows[:, bass.ds(at, CHUNK * feats)],
                                              ps_turn[k % BANKS][0:NODE_P, 0:CHUNK * feats]
                                              ).then_inc(rows_copied, 1)
                wait_alone(dve, map_copied, layer * chunks + chunks, dve_passed)

            dve.wait_ge(x_keep_in, SEM_STEP)
            x3 = x_keep[:, :].rearrange("p (c f) -> p c f", f=feats)
            settle(nc.vector.tensor_reduce(x_mean[:, :], x3, AX.X, ALU.add))
            settle(nc.vector.tensor_scalar(x_mean[:, :], x_mean[:, :], 1.0 / feats, None, ALU.mult))
            nc.vector.tensor_tensor(x3, x3, x_mean[:, :].unsqueeze(2).to_broadcast([NODE_P, cols, feats]),
                                    ALU.subtract)
            edge_phase(layers - 1)
            batch_norm(layers - 1)

            def residual(r, k):
                at = dve.snap((r * CHUNK + k) * (CHUNK * feats))
                wait_alone(dve, rows_transposed, (layers - 1) * chunks + r * CHUNK + (k + 1), dve_passed)
                nc.vector.tensor_tensor(rows[:, bass.ds(at, CHUNK * feats)],
                                        ps_turn[k % BANKS][0:NODE_P, 0:CHUNK * feats],
                                        x_keep[:, bass.ds(at, CHUNK * feats)], ALU.add).then_inc(rows_copied, 1)

            def add_squares(r, k):
                at = dve.snap((r * CHUNK + k) * CHUNK)
                wait_alone(dve, square_ready, r * CHUNK + (k + 1), dve_passed)
                nc.vector.tensor_reduce(ln_var[:, bass.ds(at, CHUNK)],
                                        ln_sq[:, k, :].rearrange("p (c f) -> p c f", f=feats), AX.X,
                                        ALU.add).then_inc(squares_added, 1)

            def layer_norm_var(r):
                at = dve.snap(r * round_cols)
                var = ln_var[:, bass.ds(at, round_cols)]
                wait_alone(dve, squares_added, r * CHUNK + CHUNK, dve_passed)
                nc.vector.tensor_scalar(var, var, 1.0 / feats, LN_EPS, ALU.mult, ALU.add).then_inc(ln_var_ready, 1)

            def layer_norm_scale(r):
                at = dve.snap(r * round_cols)
                wait_alone(dve, ln_std_ready, r + 1, dve_passed)
                std = ln_std[:, bass.ds(at, round_cols)]
                return nc.vector.reciprocal(std, std)

            for k in range(CHUNK):
                residual(0, k)
            for k in range(CHUNK):
                add_squares(0, k)
                residual(1, k)
            with dve.Fori(2, rounds) as r:
                for k in range(CHUNK):
                    add_squares(r - 1, k)
                    residual(r, k)
                    if k == 1:
                        layer_norm_var(r - 2)
                layer_norm_scale(r - 2).then_inc(ln_scale_ready, 1)
            layer_norm_var(rounds - 2)
            layer_norm_scale(rounds - 2).then_inc(ln_scale_ready, 1)
            for k in range(CHUNK):
                add_squares(rounds - 1, k)
            layer_norm_var(rounds - 1)
            settle(layer_norm_scale(rounds - 1))
            at = (rounds - 1) * round_width
            y = rows[:, at:at + round_width].rearrange("p (c f) -> p c f", f=feats)
            scale = ln_std[:, (rounds - 1) * round_cols:cols].unsqueeze(2).to_broadcast([NODE_P, round_cols, feats])
            dve.wait_ge(ln_ready, rounds - 1)
            nc.vector.tensor_tensor(y, y, scale, ALU.mult).then_inc(ln_ready, 1)


_INS = ['x', 'src', 'dst', 'edge_attr_32', 'L0_gnn_edge_w', 'L0_gnn_edge_b', 'L0_gnn_mlp_w', 'L0_gnn_mlp_b',
        'L0_gnn_gamma', 'L0_gnn_beta']


def kernel(**inputs):
    import numpy as _np
    import concourse.bacc as _bacc
    from concourse.bass_utils import run_bass_kernel_spmd as _run

    nc = _bacc.Bacc("TRN2", target_bir_lowering=False, num_devices=1)
    arrays, args = {}, []
    for name in _INS:
        a = _np.ascontiguousarray(inputs[name])
        arrays[f"in_{name}_dram"] = a
        args.append(nc.dram_tensor(f"in_{name}_dram", a.shape, mybir.dt.from_np(a.dtype), kind="ExternalInput").ap())
    out = nc.dram_tensor("out_0_dram", inputs['x'].shape, FP32, kind="ExternalOutput").ap()
    gnn_kernel(nc, *args, out)
    return _run(nc, [arrays], core_ids=[0]).results[0]["out_0_dram"]
```

```python
import concourse.bass as bass
from concourse import mybir
from contextlib import ExitStack

FP32 = mybir.dt.float32
I32 = mybir.dt.int32
ALU = mybir.AluOpType
ACT = mybir.ActivationFunctionType
AX = mybir.AxisListType

P = 128
TILES = 8
GROUP = P * TILES
RING = 8
WINDOW = 64
LOG_WINDOW = 6
HALVES = 2
NODE_P = 125
PAIRS = 2
STEPS = 5
STAGED = [(0, 2), (2, 4), (4, 5)]
BANKS = 3
BACK = [next(b for b in range(1, 2 * STEPS) if (k - b) % STEPS % BANKS == k % BANKS)
        for k in range(STEPS)]
MASKED = -32768.0
STAT_COLS = 500
BN_EPS = 1e-5
LN_EPS = 1e-5
SEM_STEP = 16


def gnn_kernel(nc, x, src, dst, edge_attr, edge_w, edge_b, mlp_w, mlp_b, gamma, beta, out):
    nodes, feats = x.shape
    edges, edge_feats = edge_attr.shape
    layers = edge_w.shape[0]
    cols = nodes // NODE_P
    step_cols = HALVES * PAIRS
    step_width = step_cols * feats
    chunks = cols // step_cols
    part = PAIRS * NODE_P
    rounds = chunks // STEPS
    round_cols = STEPS * step_cols
    round_width = STEPS * step_width
    full = edges // GROUP
    groups = full + 1
    trips = groups // RING
    tail = groups % RING
    last_edge0 = edges - GROUP
    overlap = full * GROUP - last_edge0
    blocks = -(-full // P)
    half = TILES // 2
    table_stores = rounds - 1 + STEPS
    weight_loads = half + 1 + 3 + HALVES
    assert nodes == NODE_P * step_cols * STEPS * rounds and HALVES * feats == P
    assert half * edge_feats == P and 0 <= overlap < GROUP
    assert 0 < full - (blocks - 1) * P < P and tail
    node_cols = nodes // HALVES
    window_cols = WINDOW // HALVES
    stat_parts = [(at, min(at + STAT_COLS, node_cols)) for at in range(0, node_cols, STAT_COLS)]
    padded = node_cols + window_cols

    table = nc.dram_tensor("node_table", (nodes, feats), FP32, kind="Internal").ap()
    x_rows = x.rearrange("(p c) f -> p (c f)", p=NODE_P)
    table_rows = table.rearrange("(p c) f -> p (c f)", p=NODE_P)
    out_rows = out.rearrange("(p c) f -> p (c f)", p=NODE_P)
    src_groups = src[0:full * GROUP].rearrange("(g p j) -> p g j", p=P, j=TILES)
    dst_groups = dst[0:full * GROUP].rearrange("(g p j) -> p g j", p=P, j=TILES)
    attr_groups = edge_attr[0:full * GROUP, :].rearrange("(g p j) f -> p g (j f)", p=P, j=TILES)
    src_last = src[last_edge0:edges].rearrange("(p j) -> p j", p=P)
    dst_last = dst[last_edge0:edges].rearrange("(p j) -> p j", p=P)
    attr_last = edge_attr[last_edge0:edges, :].rearrange("(p j) f -> p (j f)", p=P)

    ctx = ExitStack()
    with ctx:
        def sb(name, shape, dt=FP32):
            return ctx.enter_context(nc.sbuf_tensor(name, shape, dt))

        def sem(name):
            return ctx.enter_context(nc.semaphore(name))

        node_h = sb("node_h", [P, padded])
        rows = sb("rows", [NODE_P, cols * feats])
        x_keep = sb("x_keep", [NODE_P, cols * feats])
        ident = sb("ident", [P, P])
        centre = sb("centre", [P, P])
        fold = sb("fold", [P, feats])
        half_sum = sb("half_sum", [P, HALVES, feats])
        half_diff = sb("half_diff", [P, HALVES, feats])
        iota_nodes = sb("iota_nodes", [P, WINDOW])
        last_mask = sb("last_mask", [P, TILES])
        table_load = sb("table_load", [1, 1])
        base_all = sb("base_all", [P, groups])
        group_info = sb("group_info", [1, groups, 2], I32)
        bn_gamma = sb("bn_gamma", [P, layers])
        bn_beta = sb("bn_beta", [P, layers])
        w_edge = sb("w_edge", [P, half * feats])
        b_edge = sb("b_edge", [P, feats])
        w_mlp = sb("w_mlp", [P, P])
        w_odd = sb("w_odd", [feats, P])
        b_mlp = sb("b_mlp", [P, 1])
        src_idx = sb("src_idx", [P, RING, TILES], I32)
        dst_idx = sb("dst_idx", [P, RING, TILES], I32)
        attr = sb("attr", [P, RING, TILES * edge_feats])
        gathered = sb("gathered", [P, RING, TILES, feats])
        attr_t = sb("attr_t", [P, 2 * P])
        summed = sb("summed", [P, TILES * feats])
        messages = sb("messages", [P, TILES, feats])
        offset = sb("offset", [P, 2, TILES])
        onehot = sb("onehot", [P, 2, TILES, WINDOW])
        window_sum = sb("window_sum", [feats, HALVES, window_cols])
        stage = sb("stage", [P, STEPS, PAIRS, NODE_P])
        stats = sb("stats", [P, len(stat_parts), 6])
        mean_var = sb("mean_var", [P, 2])
        joined = sb("joined", [P, 3])
        bn_tmp = sb("bn_tmp", [P, 4])
        dst_rows = sb("dst_rows", [P, blocks + 1, GROUP], I32)
        least = sb("least", [P, blocks + 1])
        greatest = sb("greatest", [P, blocks + 1])
        shifted = sb("shifted", [P, blocks + 1], I32)
        spread_in = sb("spread_in", [P, blocks + 1, 2, P])
        x_in = sb("x_in", [NODE_P, STEPS, step_width])
        x_mean = sb("x_mean", [NODE_P, cols])
        ln_sq = sb("ln_sq", [NODE_P, STEPS, step_width])
        ln_var = sb("ln_var", [NODE_P, cols])
        ln_std = sb("ln_std", [NODE_P, cols])

        ps = ctx.enter_context(nc.psum_tensor("ps", [P, 8, 512], FP32))
        ps_embed = [ps[:, 0, :], ps[:, 1, :]]
        ps_attr = ps[:, 2, 0:2 * P]
        ps_window = ps[0:feats, 3, 0:WINDOW]
        ps_mapped = ps[:, 4, 0:window_cols]
        ps_joined = ps[:, 4, window_cols:window_cols + 3]
        window_nodes = ps[:, 7, 0:WINDOW]
        ps_map = [ps[:, k, 0:part] for k in range(BANKS)]
        ps_turn = [ps[:, 4 + k, :] for k in range(BANKS)]
        ps_base = ps[:, 3, 0:groups]
        ps_windows = ps[:, 7, WINDOW:WINDOW + groups]

        dst_rows_in = sem("dst_rows_in")
        x_in_in = [sem(f"x_in_in{k}") for k in range(STEPS)]
        x_keep_in = sem("x_keep_in")
        norm_weights_in = sem("norm_weights_in")
        weights_in = sem("weights_in")
        src_in = [sem(f"src_in{k}") for k in range(RING)]
        dst_in = [sem(f"dst_in{k}") for k in range(RING)]
        attr_in = [sem(f"attr_in{k}") for k in range(RING)]
        gather_in = [sem(f"gather_in{k}") for k in range(RING)]
        table_out = sem("table_out")
        result_out = sem("result_out")
        consts_ready = sem("consts_ready")
        x_transposed = sem("x_transposed")
        x_staged = sem("x_staged")
        x_mapped = sem("x_mapped")
        x_map_copied = sem("x_map_copied")
        bounds_ready = sem("bounds_ready")
        bounds_spread = sem("bounds_spread")
        info_ready = sem("info_ready")
        attr_transposed = sem("attr_transposed")
        attr_t_ready = sem("attr_t_ready")
        embedded = sem("embedded")
        bias_added = sem("bias_added")
        sum_ready = sem("sum_ready")
        messages_ready = sem("messages_ready")
        first_onehot_ready = sem("first_onehot_ready")
        more_onehot_ready = sem("more_onehot_ready")
        window_ready = sem("window_ready")
        window_copied = sem("window_copied")
        window_mapped = sem("window_mapped")
        edges_done = sem("edges_done")
        var_ready = sem("var_ready")
        half_stats_ready = sem("half_stats_ready")
        halves_joined = sem("halves_joined")
        std_ready = sem("std_ready")
        norm_ready = sem("norm_ready")
        staged = sem("staged")
        rows_transposed = sem("rows_transposed")
        rows_copied = sem("rows_copied")
        input_ready = sem("input_ready")
        squares_added = sem("squares_added")
        mapped = sem("mapped")
        map_copied = sem("map_copied")
        square_ready = sem("square_ready")
        ln_var_ready = sem("ln_var_ready")
        ln_std_ready = sem("ln_std_ready")
        ln_scale_ready = sem("ln_scale_ready")
        ln_ready = sem("ln_ready")
        dve_step = sem("dve_step")
        pool_step = sem("pool_step")
        sp_passed = sem("sp_passed")
        pool_passed = sem("pool_passed")
        act_passed = sem("act_passed")
        pe_passed = sem("pe_passed")
        dve_passed = sem("dve_passed")

        block = ctx.enter_context(nc.Block())

        def wait_alone(eng, s, value, passed):
            eng.wait_ge(s, value)
            eng.sem_inc(passed, 1)

        def one_ahead(eng, first, second, before_last_round=None):
            first(0, 0)
            for k in range(STEPS):
                first(k // (STEPS - 1), (k + 1) % STEPS)
                second(0, k)
            with eng.Fori(1, rounds - 1) as r:
                for k in range(STEPS):
                    first(r + k // (STEPS - 1), (k + 1) % STEPS)
                    second(r, k)
            if before_last_round:
                before_last_round()
            for k in range(STEPS):
                if k < STEPS - 1:
                    first(rounds - 1, k + 1)
                second(rounds - 1, k)

        def reused(r, k, slots):
            return not isinstance(r, int) or r > 0 or k >= slots

        def slot_count(layer, i, k):
            return layer * (trips + (k < tail)) + i

        by_pair = node_h[:, 0:node_cols].rearrange("h (p q) -> h q p", p=NODE_P)

        @block.sync
        def _(sp):
            def load_weights(layer):
                w = edge_w[bass.ds(layer, 1), :, :].rearrange("o k f -> (o k) f")
                for q in range(half):
                    sp.dma_start(w_edge[q * edge_feats:(q + 1) * edge_feats, q * feats:(q + 1) * feats],
                                 w).then_inc(weights_in, SEM_STEP)
                sp.dma_start(b_edge[:, :], edge_b[bass.ds(layer, 1), :].to_broadcast([P, feats])
                             ).then_inc(weights_in, SEM_STEP)
                w = mlp_w[bass.ds(layer, 1), :, :].rearrange("o k f -> (o k) f")
                sp.dma_start(w_mlp[0:feats, 0:feats], w).then_inc(weights_in, SEM_STEP)
                sp.dma_start(w_mlp[feats:P, feats:P], w).then_inc(weights_in, SEM_STEP)
                sp.dma_start(w_odd[:, feats:P], w).then_inc(weights_in, SEM_STEP)
                for h in range(HALVES):
                    sp.dma_start(b_mlp[h * feats:(h + 1) * feats, :],
                                 mlp_b[bass.ds(layer, 1), :].rearrange("o f -> f o"),
                                 allow_slow_non_contiguous=True).then_inc(weights_in, SEM_STEP)

            def load_group(k, s, d, a):
                sp.dma_start(src_idx[:, k, :], s).then_inc(src_in[k], SEM_STEP)
                sp.dma_start(dst_idx[:, k, :], d).then_inc(dst_in[k], SEM_STEP)
                sp.dma_start(attr[:, k, :], a).then_inc(attr_in[k], SEM_STEP)

            def group_of(view, g):
                return view[:, bass.ds(g, 1), :].rearrange("p o n -> p (o n)")

            def wait_slot(layer, i, k):
                wait_alone(sp, gather_in[k], slot_count(layer, i, k) * (SEM_STEP * TILES), sp_passed)
                wait_alone(sp, attr_transposed, layer * groups + i * RING + (k - RING + 1), sp_passed)
                wait_alone(sp, sum_ready, layer * groups + i * RING + (k - RING + 1), sp_passed)

            def first_groups(some):
                for k in some:
                    load_group(k, src_groups[:, k, :], dst_groups[:, k, :], attr_groups[:, k, :])

            def later_groups(layer):
                with sp.Fori(1, trips) as i:
                    for k in range(RING):
                        g = sp.snap(i * RING + k)
                        wait_slot(layer, i, k)
                        load_group(k, group_of(src_groups, g), group_of(dst_groups, g), group_of(attr_groups, g))
                for k in range(tail):
                    g = trips * RING + k
                    wait_slot(layer, trips, k)
                    if g < full:
                        load_group(k, src_groups[:, g, :], dst_groups[:, g, :], attr_groups[:, g, :])
                    else:
                        load_group(k, src_last, dst_last, attr_last)

            first_groups([0])
            for k in range(STEPS):
                sp.dma_start(x_in[:, k, :], x_rows[:, k * step_width:(k + 1) * step_width]).then_inc(x_in_in[k], SEM_STEP)
            sp.wait_ge(consts_ready, 1)
            load_weights(0)
            first_groups([1])
            for b in range(blocks):
                n = min(P, full - b * P)
                sp.dma_start(dst_rows[0:n, b, :],
                             dst[b * P * GROUP:(b * P + n) * GROUP].rearrange("(g e) -> g e", e=GROUP)
                             ).then_inc(dst_rows_in, SEM_STEP)
            sp.dma_start(dst_rows[0:1, blocks, :],
                         dst[last_edge0:edges].rearrange("(o e) -> o e", o=1)).then_inc(dst_rows_in, SEM_STEP)
            first_groups(range(2, RING))
            with sp.Fori(1, rounds) as r:
                for k in range(STEPS):
                    at = sp.snap((r * STEPS + k) * step_width)
                    wait_alone(sp, x_transposed, r * STEPS + (k - STEPS + 1), sp_passed)
                    sp.dma_start(x_in[:, k, :], x_rows[:, bass.ds(at, step_width)]).then_inc(x_in_in[k], SEM_STEP)
            for h in range(HALVES):
                sp.dma_start(bn_gamma[h * feats:(h + 1) * feats, :], gamma.rearrange("l f -> f l"),
                             allow_slow_non_contiguous=True).then_inc(norm_weights_in, SEM_STEP)
                sp.dma_start(bn_beta[h * feats:(h + 1) * feats, :], beta.rearrange("l f -> f l"),
                             allow_slow_non_contiguous=True).then_inc(norm_weights_in, SEM_STEP)
            sp.dma_start(x_keep[:, :], x_rows).then_inc(x_keep_in, SEM_STEP)

            with sp.Fori(0, layers - 1) as layer:
                later_groups(layer)
                wait_alone(sp, edges_done, layer + 1, sp_passed)
                first_groups(range(RING))
                load_weights(layer + 1)
                with sp.Fori(0, rounds - 1) as r:
                    at = sp.snap(r * round_width)
                    wait_alone(sp, rows_copied, layer * chunks + r * STEPS + STEPS, sp_passed)
                    sp.dma_start(table_rows[:, bass.ds(at, round_width)],
                                 rows[:, bass.ds(at, round_width)]).then_inc(table_out, SEM_STEP)
                for k in range(STEPS):
                    at = (rounds - 1) * round_width + k * step_width
                    wait_alone(sp, rows_copied, layer * chunks + (rounds - 1) * STEPS + k + 1, sp_passed)
                    sp.dma_start(table_rows[:, at:at + step_width],
                                 rows[:, at:at + step_width]).then_inc(table_out, SEM_STEP)
            later_groups(layers - 1)

            with sp.Fori(0, rounds) as r:
                at = sp.snap(r * round_width)
                wait_alone(sp, ln_ready, r + 1, sp_passed)
                sp.dma_start(out_rows[:, bass.ds(at, round_width)],
                             rows[:, bass.ds(at, round_width)]).then_inc(result_out, SEM_STEP)
            sp.wait_ge(table_out, SEM_STEP * table_stores * (layers - 1))
            sp.wait_ge(result_out, SEM_STEP * rounds)

        @block.gpsimd
        def _(pool):
            nc.gpsimd.memset(w_mlp[:, :], 0.0)
            nc.gpsimd.memset(w_odd[:, :], 0.0)
            nc.gpsimd.memset(w_edge[:, :], 0.0).then_inc(consts_ready, 1)
            nc.gpsimd.memset(last_mask[:, :], 0.0)
            nc.gpsimd.iota(iota_nodes[:, :], [[1, WINDOW]], base=0, channel_multiplier=0,
                           allow_small_or_imprecise_dtypes=True)
            nc.gpsimd.memset(ident[:, :], 0.0).then_inc(pool_step, 1)
            pool.wait_ge(pool_step, 1)
            nc.gpsimd.affine_select(out=ident[:, :], in_=ident[:, :], pattern=[[-1, P]],
                                    compare_op=ALU.not_equal, fill=1.0, base=0, channel_multiplier=1)
            nc.gpsimd.affine_select(out=last_mask[:, :], in_=last_mask[:, :], pattern=[[1, TILES]],
                                    compare_op=ALU.is_ge, fill=MASKED, base=-overlap,
                                    channel_multiplier=TILES).then_inc(consts_ready, 1)

            last_node = pool.to_reg(nodes - 1)

            def gather_group(features, layer, i, k, wait):
                wait_alone(pool, src_in[k], slot_count(layer, i, k) * SEM_STEP + SEM_STEP, pool_passed)
                if wait:
                    wait_alone(pool, sum_ready, layer * groups + i * RING + (k - RING + 1), pool_passed)
                for j in range(TILES):
                    pool.indirect_dma_start(
                        out=gathered[:, k, j, :], out_offset=None, in_=features,
                        in_offset=bass.IndirectOffsetOnAxis(ap=src_idx[:, k, j:j + 1], axis=0),
                        bounds_check=last_node).then_inc(gather_in[k], SEM_STEP)

            def layer_gathers(layer, features):
                for k in range(RING):
                    gather_group(features, layer, 0, k, False)
                with pool.Fori(1, trips) as i:
                    for k in range(RING):
                        gather_group(features, layer, i, k, True)
                for k in range(tail):
                    gather_group(features, layer, trips, k, True)

            layer_gathers(0, x[:, :])
            with pool.Fori(1, layers) as layer:
                wait_alone(pool, table_out, layer * (SEM_STEP * table_stores), pool_passed)
                layer_gathers(layer, table[:, :])

            with pool.Fori(0, rounds - 1) as r:
                at = pool.snap(r * round_width)
                at_col = pool.snap(r * round_cols)
                wait_alone(pool, ln_scale_ready, r + 1, pool_passed)
                y = rows[:, bass.ds(at, round_width)].rearrange("p (c f) -> p c f", f=feats)
                scale = ln_std[:, bass.ds(at_col, round_cols)].unsqueeze(2).to_broadcast([NODE_P, round_cols, feats])
                nc.gpsimd.tensor_tensor(y, y, scale, ALU.mult).then_inc(ln_ready, 1)

        @block.scalar
        def _(act):
            def stage_x(r, k):
                wait_alone(act, x_transposed, r * STEPS + (k + 1), act_passed)
                if reused(r, k, STEPS):
                    wait_alone(act, x_mapped, r * STEPS + (k - STEPS + 1), act_passed)
                nc.scalar.copy(stage[:, k, :, :].rearrange("h q p -> h (q p)"),
                               ps_turn[k % BANKS][:, 0:part]).then_inc(x_staged, 1)

            def copy_x_map(r, k):
                at = act.snap((r * STEPS + k) * PAIRS)
                wait_alone(act, x_mapped, r * STEPS + (k + 1), act_passed)
                nc.scalar.activation(by_pair[:, bass.ds(at, PAIRS), :],
                                     ps_map[k % BANKS].rearrange("h (q p) -> h q p", q=PAIRS), ACT.Identity,
                                     bias=b_mlp[:, :]).then_inc(x_map_copied, 1)

            def copy_attr(n):
                wait_alone(act, attr_transposed, n + 1, act_passed)
                nc.scalar.copy(attr_t[:, :], ps_attr).then_inc(attr_t_ready, 1)

            def relu_messages(n):
                wait_alone(act, sum_ready, n + 1, act_passed)
                nc.scalar.activation(messages[:, :, :].rearrange("p j f -> p (j f)"), summed[:, :],
                                     ACT.Relu).then_inc(messages_ready, 1)

            def edge_phase(layer):
                copy_attr(layer * groups)
                with act.Fori(0, trips) as i:
                    for k in range(RING):
                        n = layer * groups + i * RING + k
                        copy_attr(n + 1)
                        relu_messages(n)
                for k in range(tail):
                    n = layer * groups + trips * RING + k
                    if k < tail - 1:
                        copy_attr(n + 1)
                    relu_messages(n)

            def normalise(layer, r, steps):
                start, end = steps
                at = act.snap((r * STEPS + start) * PAIRS)
                if reused(r, start, STEPS):
                    wait_alone(act, rows_transposed, layer * chunks + r * STEPS + (end - STEPS), act_passed)
                nc.scalar.activation(stage[:, start:end, :, :].rearrange("h k q p -> h (k q) p"),
                                     by_pair[:, bass.ds(at, (end - start) * PAIRS), :], ACT.Relu,
                                     bias=bn_tmp[:, 3:4], scale=bn_tmp[:, 2:3]).then_inc(staged, 1)

            def normalise_in_place(r, k):
                at = act.snap((r * STEPS + k) * part)
                nc.scalar.activation(node_h[:, bass.ds(at, part)], node_h[:, bass.ds(at, part)],
                                     ACT.Relu, bias=bn_tmp[:, 3:4], scale=bn_tmp[:, 2:3]).then_inc(input_ready, 1)

            def square(r, k):
                at = act.snap((r * STEPS + k) * step_width)
                wait_alone(act, rows_copied, (layers - 1) * chunks + r * STEPS + (k + 1), act_passed)
                nc.scalar.activation(ln_sq[:, k, :], rows[:, bass.ds(at, step_width)],
                                     ACT.Square).then_inc(square_ready, 1)

            def batch_scale(layer):
                wait_alone(act, var_ready, layer + 1, act_passed)
                nc.scalar.activation(bn_tmp[:, 1:2], bn_tmp[:, 0:1], ACT.Sqrt).then_inc(std_ready, 1)
                wait_alone(act, norm_ready, layer + 1, act_passed)

            def layer_norm_std(r):
                at = act.snap(r * round_cols)
                wait_alone(act, ln_var_ready, r + 1, act_passed)
                nc.scalar.activation(ln_std[:, bass.ds(at, round_cols)], ln_var[:, bass.ds(at, round_cols)],
                                     ACT.Sqrt).then_inc(ln_std_ready, 1)

            act.wait_ge(consts_ready, 2)
            nc.scalar.activation(table_load[:, :], ident[0:1, 0:1], ACT.Sqrt)
            one_ahead(act, stage_x, copy_x_map)

            with act.Fori(0, layers - 1) as layer:
                edge_phase(layer)
                batch_scale(layer)
                for steps in STAGED:
                    normalise(layer, 0, steps)
                with act.Fori(1, rounds) as r:
                    for steps in STAGED:
                        normalise(layer, r, steps)

                def copy_map(r, k):
                    at = act.snap((r * STEPS + k) * part)
                    wait_alone(act, mapped, layer * chunks + r * STEPS + (k + 1), act_passed)
                    nc.scalar.activation(node_h[:, bass.ds(at, part)], ps_map[k % BANKS], ACT.Identity,
                                         bias=b_mlp[:, :]).then_inc(map_copied, 1)

                wait_alone(act, staged, (layer + 1) * rounds * len(STAGED), act_passed)
                one_ahead(act, normalise_in_place, copy_map)

            edge_phase(layers - 1)
            batch_scale(layers - 1)
            for steps in STAGED:
                normalise(layers - 1, 0, steps)
            for steps in STAGED:
                for k in range(*steps):
                    square(0, k)
                normalise(layers - 1, 1, steps)
            with act.Fori(2, rounds) as r:
                for steps in STAGED:
                    for k in range(*steps):
                        square(r - 1, k)
                    normalise(layers - 1, r, steps)
                    if steps == STAGED[0]:
                        layer_norm_std(r - 2)
            for k in range(STEPS):
                square(rounds - 1, k)
                if k == 1:
                    layer_norm_std(rounds - 2)
            layer_norm_std(rounds - 1)

        @block.tensor
        def _(pe):
            pe.wait_ge(consts_ready, 2)

            def transpose_x(r, k):
                wait_alone(pe, x_in_in[k], r * SEM_STEP + SEM_STEP, pe_passed)
                if reused(r, k, BANKS):
                    wait_alone(pe, x_staged, r * STEPS + (k - BACK[k] + 1), pe_passed)
                for q in range(PAIRS):
                    last = nc.tensor.transpose(ps_turn[k % BANKS][:, q * NODE_P:(q + 1) * NODE_P],
                                               x_in[:, k, q * P:(q + 1) * P],
                                               ident[0:NODE_P, 0:NODE_P])
                last.then_inc(x_transposed, 1)

            def map_x(r, k):
                wait_alone(pe, x_staged, r * STEPS + (k + 1), pe_passed)
                if reused(r, k, BANKS):
                    wait_alone(pe, x_map_copied, r * STEPS + (k - BACK[k] + 1), pe_passed)
                elif k == 0:
                    pe.wait_ge(weights_in, SEM_STEP * weight_loads)
                nc.tensor.matmul(ps_map[k % BANKS], w_mlp[:, :],
                                 stage[:, k, :, :].rearrange("h q p -> h (q p)"),
                                 start=True, stop=True).then_inc(x_mapped, 1)

            def spread_bounds():
                pe.wait_ge(bounds_ready, 1)
                for b in range(blocks + 1):
                    n = min(P, full - b * P) if b < blocks else 1
                    at = b * P if b < blocks else full
                    nc.tensor.matmul(ps_base[:, at:at + n], spread_in[0:n, b, 0, :], ident[0:n, 0:n],
                                     start=True, stop=True)
                    nc.tensor.matmul(ps_windows[:, at:at + n], spread_in[0:n, b, 1, :], ident[0:n, 0:n],
                                     start=True, stop=True).then_inc(bounds_spread, 1)

            one_ahead(pe, transpose_x, map_x, spread_bounds)

            def embed(n, layer, i, k):
                wait_alone(pe, attr_in[k], slot_count(layer, i, k) * SEM_STEP + SEM_STEP, pe_passed)
                for q in range(2):
                    last = nc.tensor.transpose(ps_attr[:, q * P:(q + 1) * P], attr[:, k, q * P:(q + 1) * P],
                                               ident[:, :])
                last.then_inc(attr_transposed, 1)
                wait_alone(pe, attr_t_ready, n + 1, pe_passed)
                width = half * feats
                for q in range(2):
                    last = nc.tensor.matmul(ps_embed[k % 2][:, q * width:(q + 1) * width],
                                            attr_t[:, q * P:(q + 1) * P], w_edge[:, :], start=True, stop=True)
                last.then_inc(embedded, 1)

            windows = pe.alloc_register("pe_windows")
            pe.reg_mov(windows, 0)
            more_windows = pe.alloc_register("pe_more_windows")
            pe.reg_mov(more_windows, 0)

            def sum_window(k):
                pe.reg_add(windows, windows, 1)
                windows_now = pe.snap(windows, min_val=1, max_val=1 << 30)
                for j in range(TILES):
                    last = nc.tensor.matmul(ps_window, messages[:, j, :], onehot[:, k % 2, j, :],
                                            start=(j == 0), stop=(j == TILES - 1))
                last.then_inc(window_ready, 1)
                wait_alone(pe, window_copied, windows_now, pe_passed)
                nc.tensor.matmul(ps_mapped, w_mlp[0:feats, :], window_sum[:, 0, :], start=True, stop=False)
                nc.tensor.matmul(ps_mapped, w_odd[:, :], window_sum[:, 1, :],
                                 start=False, stop=True).then_inc(window_mapped, 1)

            def sum_windows(n, k, g):
                count = pe.value_load(group_info[0:1, bass.ds(g, 1), 1], min_val=1, max_val=nodes // WINDOW + 1)
                wait_alone(pe, first_onehot_ready, n + 1, pe_passed)
                wait_alone(pe, messages_ready, n + 1, pe_passed)
                sum_window(k)
                with pe.If(count > 1), pe.Fori(1, count):
                    pe.reg_add(more_windows, more_windows, 1)
                    wait_alone(pe, more_onehot_ready, pe.snap(more_windows, min_val=1, max_val=1 << 30), pe_passed)
                    sum_window(k)

            def edge_phase(layer):
                wait_alone(pe, weights_in, layer * (SEM_STEP * weight_loads) + SEM_STEP * weight_loads, pe_passed)
                embed(layer * groups, layer, 0, 0)
                with pe.Fori(0, trips) as i:
                    for k in range(RING):
                        n = layer * groups + i * RING + k
                        if k < RING - 1:
                            embed(n + 1, layer, i, k + 1)
                        else:
                            embed(n + 1, layer, i + 1, 0)
                        sum_windows(n, k, i * RING + k)
                for k in range(tail):
                    n = layer * groups + trips * RING + k
                    if k < tail - 1:
                        embed(n + 1, layer, trips, k + 1)
                    sum_windows(n, k, trips * RING + k)
                wait_alone(pe, edges_done, layer + 1, pe_passed)

            def to_rows(layer, r, k, turn):
                part_of_k = next(m for m, (start, end) in enumerate(STAGED) if k < end)
                wait_alone(pe, staged, (layer * rounds + r) * len(STAGED) + part_of_k + 1, pe_passed)
                if reused(r, k, BANKS):
                    wait_alone(pe, rows_copied, layer * chunks + r * STEPS + (k - BACK[k] + 1), pe_passed)
                for q in range(PAIRS):
                    last = turn(ps_turn[k % BANKS][0:NODE_P, q * P:(q + 1) * P], stage[:, k, q, :])
                last.then_inc(rows_transposed, 1)

            def node_phase(layer, turn):
                for k in range(STEPS):
                    to_rows(layer, 0, k, turn)
                with pe.Fori(1, rounds) as r:
                    for k in range(STEPS):
                        to_rows(layer, r, k, turn)

            def transpose_chunk(to, nodes_t):
                return nc.tensor.transpose(to, nodes_t, ident[:, :])

            def centre_chunk(to, nodes_t):
                return nc.tensor.matmul(to, nodes_t, centre[:, :], start=True, stop=True)

            def join_halves(layer):
                wait_alone(pe, half_stats_ready, layer + 1, pe_passed)
                nc.tensor.matmul(ps_joined[:, 0:2], half_sum[:, :, :].rearrange("p h f -> p (h f)"), mean_var[:, :],
                                 start=True, stop=True)
                nc.tensor.matmul(ps_joined[:, 2:3], half_diff[:, :, :].rearrange("p h f -> p (h f)"),
                                 mean_var[:, 0:1], start=True, stop=True).then_inc(halves_joined, 1)

            def map_nodes(layer, r, k):
                at = pe.snap((r * STEPS + k) * part)
                wait_alone(pe, input_ready, layer * chunks + r * STEPS + (k + 1), pe_passed)
                if reused(r, k, BANKS):
                    wait_alone(pe, map_copied, layer * chunks + r * STEPS + (k - BACK[k] + 1), pe_passed)
                nc.tensor.matmul(ps_map[k % BANKS], w_mlp[:, :], node_h[:, bass.ds(at, part)],
                                 start=True, stop=True).then_inc(mapped, 1)

            pe.wait_ge(info_ready, 1)
            pe.wait_ge(x_map_copied, chunks)
            with pe.Fori(0, layers - 1) as layer:
                edge_phase(layer)
                join_halves(layer)
                node_phase(layer, transpose_chunk)
                wait_alone(pe, weights_in, (layer + 1) * (SEM_STEP * weight_loads) + SEM_STEP * weight_loads,
                           pe_passed)
                for k in range(STEPS):
                    map_nodes(layer, 0, k)
                with pe.Fori(1, rounds) as r:
                    for k in range(STEPS):
                        map_nodes(layer, r, k)
                wait_alone(pe, map_copied, layer * chunks + chunks, pe_passed)
            edge_phase(layers - 1)
            join_halves(layers - 1)
            node_phase(layers - 1, centre_chunk)

        @block.vector
        def _(dve):
            steps = dve.alloc_register("dve_steps")
            dve.reg_mov(steps, 0)

            def settle(instruction):
                instruction.then_inc(dve_step, 1)
                dve.reg_add(steps, steps, 1)
                wait_alone(dve, dve_step, dve.snap(steps, min_val=1, max_val=1 << 30), dve_passed)

            nc.vector.memset(node_h[:, node_cols:padded], 0.0)
            nc.vector.memset(least[:, :], 0.0)
            nc.vector.memset(greatest[:, :], 0.0)
            dve.wait_ge(consts_ready, 2)
            nc.vector.tensor_copy(window_nodes, iota_nodes[:, :])
            for h in range(HALVES):
                for g in range(HALVES):
                    last = nc.vector.memset(centre[h * feats:(h + 1) * feats, g * feats:(g + 1) * feats],
                                            -1.0 / feats if g == h else 0.0)
            settle(last)
            nc.vector.tensor_tensor(centre[:, :], centre[:, :], ident[:, :], ALU.add)
            settle(nc.vector.tensor_tensor(fold[:, :], ident[:, 0:feats], ident[:, feats:P], ALU.add))
            folds = fold[:, :].unsqueeze(1).to_broadcast([P, HALVES, feats])
            nc.vector.tensor_scalar(half_sum[:, :, :], folds, 0.5, None, ALU.mult)
            nc.vector.tensor_scalar(half_diff[0:feats, :, :], folds[0:feats], 0.5, None, ALU.mult)
            nc.vector.tensor_scalar(half_diff[feats:P, :, :], folds[feats:P], -0.5, None, ALU.mult)
            dve.wait_ge(dst_rows_in, SEM_STEP * (blocks + 1))
            for b in range(blocks + 1):
                n = min(P, full - b * P) if b < blocks else 1
                nc.vector.tensor_reduce(least[0:n, b:b + 1], dst_rows[0:n, b, :], AX.X, ALU.min)
                last = nc.vector.tensor_reduce(greatest[0:n, b:b + 1], dst_rows[0:n, b, :], AX.X, ALU.max)
            settle(last)
            settle(nc.vector.tensor_copy(shifted[:, :], least[:, :]))
            settle(nc.vector.tensor_scalar(shifted[:, :], shifted[:, :], 1, None, ALU.logical_shift_right))
            nc.vector.tensor_copy(spread_in[:, :, 0, :], shifted[:, :].unsqueeze(2).to_broadcast([P, blocks + 1, P]))
            settle(nc.vector.tensor_scalar(least[:, :], shifted[:, :], 2.0, None, ALU.mult))
            settle(nc.vector.tensor_tensor(shifted[:, :], greatest[:, :], least[:, :], ALU.subtract))
            settle(nc.vector.tensor_scalar(shifted[:, :], shifted[:, :], LOG_WINDOW, None, ALU.logical_shift_right))
            settle(nc.vector.tensor_scalar(greatest[:, :], shifted[:, :], 1.0, None, ALU.add))
            nc.vector.tensor_copy(spread_in[:, :, 1, :],
                                  greatest[:, :].unsqueeze(2).to_broadcast([P, blocks + 1, P])
                                  ).then_inc(bounds_ready, 1)
            dve.wait_ge(bounds_spread, blocks + 1)
            nc.vector.tensor_scalar(base_all[:, :], ps_base, 2.0, None, ALU.mult)
            nc.vector.tensor_copy(group_info[0:1, :, 0], ps_base[0:1, :])
            nc.vector.tensor_copy(group_info[0:1, :, 1], ps_windows[0:1, :]).then_inc(info_ready, 1)
            dve.wait_ge(info_ready, 1)

            windows = dve.alloc_register("dve_windows")
            dve.reg_mov(windows, 0)

            def make_onehot(k):
                return nc.vector.tensor_tensor(onehot[:, k % 2, :, :],
                                               window_nodes.unsqueeze(1).to_broadcast([P, TILES, WINDOW]),
                                               offset[:, k % 2, :].unsqueeze(2).to_broadcast([P, TILES, WINDOW]),
                                               ALU.is_equal)

            def prepare(layer, i, k, g, last_group=False):
                wait_alone(dve, dst_in[k], slot_count(layer, i, k) * SEM_STEP + SEM_STEP, dve_passed)
                settle(nc.vector.tensor_scalar(offset[:, k % 2, :], dst_idx[:, k, :], base_all[:, bass.ds(g, 1)], None,
                                               ALU.subtract))
                if last_group:
                    settle(nc.vector.tensor_tensor(offset[:, k % 2, :], offset[:, k % 2, :], last_mask[:, :], ALU.add))
                make_onehot(k).then_inc(first_onehot_ready, 1)
                wait_alone(dve, embedded, layer * groups + g + 1, dve_passed)
                embeddings = ps_embed[k % 2].rearrange("p (j f) -> p j f", f=feats)
                nc.vector.tensor_tensor(embeddings, embeddings,
                                        b_edge[:, :].unsqueeze(1).to_broadcast([P, TILES, feats]),
                                        ALU.add).then_inc(bias_added, 1)

            def add_window(at):
                dve.reg_add(windows, windows, 1)
                windows_now = dve.snap(windows, min_val=1, max_val=1 << 30)
                wait_alone(dve, window_ready, windows_now, dve_passed)
                nc.vector.tensor_copy(window_sum[:, :, :], ps_window.rearrange("f (n h) -> f h n", h=HALVES)
                                      ).then_inc(window_copied, 1)
                wait_alone(dve, window_mapped, windows_now, dve_passed)
                settle(nc.vector.tensor_tensor(node_h[:, bass.ds(at, window_cols)],
                                               node_h[:, bass.ds(at, window_cols)], ps_mapped, ALU.add))

            def group(layer, i, k, g, prepare_next=None):
                n = layer * groups + g
                wait_alone(dve, bias_added, n + 1, dve_passed)
                wait_alone(dve, gather_in[k],
                           slot_count(layer, i, k) * (SEM_STEP * TILES) + SEM_STEP * TILES, dve_passed)
                nc.vector.tensor_tensor(summed[:, :], ps_embed[k % 2],
                                        gathered[:, k, :, :].rearrange("p j f -> p (j f)"),
                                        ALU.add).then_inc(sum_ready, 1)
                if prepare_next:
                    prepare_next()
                base = dve.value_load(group_info[0:1, bass.ds(g, 1), 0], min_val=0, max_val=node_cols - 1)
                count = dve.value_load(group_info[0:1, bass.ds(g, 1), 1], min_val=1, max_val=nodes // WINDOW + 1)
                add_window(base)
                with dve.If(count > 1), dve.Fori(1, count) as w:
                    settle(nc.vector.tensor_scalar(offset[:, k % 2, :], offset[:, k % 2, :], float(WINDOW), None,
                                                   ALU.subtract))
                    make_onehot(k).then_inc(more_onehot_ready, 1)
                    add_window(nc.s_assert_within(
                        dve.snap(base + w * window_cols), 0, node_cols - 1,
                        skip_runtime_bounds_check_because="the last window holds a destination"))

            def edge_phase(layer):
                prepare(layer, 0, 0, 0)
                with dve.Fori(0, trips) as i:
                    for k in range(RING):
                        j, next_k = (i, k + 1) if k < RING - 1 else (i + 1, 0)
                        group(layer, i, k, i * RING + k, lambda: prepare(layer, j, next_k, i * RING + (k + 1)))
                for k in range(tail):
                    g = trips * RING + k
                    if k < tail - 1:
                        group(layer, trips, k, g,
                              lambda: prepare(layer, trips, k + 1, g + 1, last_group=(k == tail - 2)))
                    else:
                        group(layer, trips, k, g)
                dve.sem_inc(edges_done, 1)

            def batch_norm(layer):
                for m, (start, end) in enumerate(stat_parts):
                    last = nc.vector.bn_stats(stats[:, m, :], node_h[:, start:end])
                settle(last)
                nc.vector.bn_aggr(mean_var[:, :], stats[:, :, :].rearrange("f c s -> f (c s)")
                                  ).then_inc(half_stats_ready, 1)
                wait_alone(dve, halves_joined, layer + 1, dve_passed)
                settle(nc.vector.tensor_copy(joined[:, :], ps_joined))
                settle(nc.vector.tensor_tensor(joined[:, 2:3], joined[:, 2:3], joined[:, 2:3], ALU.mult))
                settle(nc.vector.tensor_tensor(bn_tmp[:, 0:1], joined[:, 1:2], joined[:, 2:3], ALU.add))
                nc.vector.tensor_scalar(bn_tmp[:, 0:1], bn_tmp[:, 0:1], BN_EPS, None, ALU.add).then_inc(var_ready, 1)
                wait_alone(dve, std_ready, layer + 1, dve_passed)
                settle(nc.vector.reciprocal(bn_tmp[:, 1:2], bn_tmp[:, 1:2]))
                settle(nc.vector.tensor_tensor(bn_tmp[:, 2:3], bn_tmp[:, 1:2], bn_gamma[:, bass.ds(layer, 1)],
                                               ALU.mult))
                settle(nc.vector.tensor_tensor(bn_tmp[:, 0:1], joined[:, 0:1], bn_tmp[:, 2:3], ALU.mult))
                nc.vector.tensor_tensor(bn_tmp[:, 3:4], bn_beta[:, bass.ds(layer, 1)], bn_tmp[:, 0:1],
                                        ALU.subtract).then_inc(norm_ready, 1)

            dve.wait_ge(norm_weights_in, 2 * HALVES * SEM_STEP)
            dve.wait_ge(x_map_copied, chunks)
            with dve.Fori(0, layers - 1) as layer:
                edge_phase(layer)
                batch_norm(layer)
                with dve.Fori(0, rounds) as r:
                    for k in range(STEPS):
                        at = dve.snap((r * STEPS + k) * step_width)
                        wait_alone(dve, rows_transposed, layer * chunks + r * STEPS + (k + 1), dve_passed)
                        nc.vector.tensor_copy(rows[:, bass.ds(at, step_width)],
                                              ps_turn[k % BANKS][0:NODE_P, 0:step_width]
                                              ).then_inc(rows_copied, 1)
                wait_alone(dve, map_copied, layer * chunks + chunks, dve_passed)

            dve.wait_ge(x_keep_in, SEM_STEP)
            x3 = x_keep[:, :].rearrange("p (c f) -> p c f", f=feats)
            settle(nc.vector.tensor_reduce(x_mean[:, :], x3, AX.X, ALU.add))
            settle(nc.vector.tensor_scalar(x_mean[:, :], x_mean[:, :], 1.0 / feats, None, ALU.mult))
            nc.vector.tensor_tensor(x3, x3, x_mean[:, :].unsqueeze(2).to_broadcast([NODE_P, cols, feats]),
                                    ALU.subtract)
            edge_phase(layers - 1)
            batch_norm(layers - 1)

            def residual(r, k):
                at = dve.snap((r * STEPS + k) * step_width)
                wait_alone(dve, rows_transposed, (layers - 1) * chunks + r * STEPS + (k + 1), dve_passed)
                nc.vector.tensor_tensor(rows[:, bass.ds(at, step_width)],
                                        ps_turn[k % BANKS][0:NODE_P, 0:step_width],
                                        x_keep[:, bass.ds(at, step_width)], ALU.add).then_inc(rows_copied, 1)

            def add_squares(r, k):
                at = dve.snap((r * STEPS + k) * step_cols)
                wait_alone(dve, square_ready, r * STEPS + (k + 1), dve_passed)
                nc.vector.tensor_reduce(ln_var[:, bass.ds(at, step_cols)],
                                        ln_sq[:, k, :].rearrange("p (c f) -> p c f", f=feats), AX.X,
                                        ALU.add).then_inc(squares_added, 1)

            def layer_norm_var(r):
                at = dve.snap(r * round_cols)
                var = ln_var[:, bass.ds(at, round_cols)]
                wait_alone(dve, squares_added, r * STEPS + STEPS, dve_passed)
                nc.vector.tensor_scalar(var, var, 1.0 / feats, LN_EPS, ALU.mult, ALU.add).then_inc(ln_var_ready, 1)

            def layer_norm_scale(r):
                at = dve.snap(r * round_cols)
                wait_alone(dve, ln_std_ready, r + 1, dve_passed)
                std = ln_std[:, bass.ds(at, round_cols)]
                return nc.vector.reciprocal(std, std)

            for k in range(STEPS):
                residual(0, k)
            for k in range(STEPS):
                add_squares(0, k)
                residual(1, k)
            with dve.Fori(2, rounds) as r:
                layer_norm_var(r - 2)
                for k in range(STEPS):
                    add_squares(r - 1, k)
                    residual(r, k)
                    if k == 3:
                        layer_norm_scale(r - 2).then_inc(ln_scale_ready, 1)
            layer_norm_var(rounds - 2)
            for k in range(STEPS):
                add_squares(rounds - 1, k)
                if k == 2:
                    layer_norm_scale(rounds - 2).then_inc(ln_scale_ready, 1)
            layer_norm_var(rounds - 1)
            settle(layer_norm_scale(rounds - 1))
            at = (rounds - 1) * round_width
            y = rows[:, at:at + round_width].rearrange("p (c f) -> p c f", f=feats)
            scale = ln_std[:, (rounds - 1) * round_cols:cols].unsqueeze(2).to_broadcast([NODE_P, round_cols, feats])
            dve.wait_ge(ln_ready, rounds - 1)
            nc.vector.tensor_tensor(y, y, scale, ALU.mult).then_inc(ln_ready, 1)


_INS = ['x', 'src', 'dst', 'edge_attr_32', 'L0_gnn_edge_w', 'L0_gnn_edge_b', 'L0_gnn_mlp_w', 'L0_gnn_mlp_b',
        'L0_gnn_gamma', 'L0_gnn_beta']


def kernel(**inputs):
    import numpy as _np
    import concourse.bacc as _bacc
    from concourse.bass_utils import run_bass_kernel_spmd as _run

    nc = _bacc.Bacc("TRN2", target_bir_lowering=False, num_devices=1)
    arrays, args = {}, []
    for name in _INS:
        a = _np.ascontiguousarray(inputs[name])
        arrays[f"in_{name}_dram"] = a
        args.append(nc.dram_tensor(f"in_{name}_dram", a.shape, mybir.dt.from_np(a.dtype), kind="ExternalInput").ap())
    out = nc.dram_tensor("out_0_dram", inputs['x'].shape, FP32, kind="ExternalOutput").ap()
    gnn_kernel(nc, *args, out)
    return _run(nc, [arrays], core_ids=[0]).results[0]["out_0_dram"]
```
